# Optimizing a Trainium2 kernel written in Bass

```python
import numpy as np
import jax
import jax.numpy as jnp

def _softmax(x, axis=-1):
    return jax.nn.softmax(x, axis=axis)

def _gelu(x):
    return jax.nn.gelu(x, approximate=True)

def _silu(x):
    return jax.nn.silu(x)

def _sigmoid(x):
    return jax.nn.sigmoid(x)

def _layernorm(x, axis=-1, eps=1e-05):
    m = jnp.mean(x, axis=axis, keepdims=True)
    v = jnp.var(x, axis=axis, keepdims=True)
    return (x - m) / jnp.sqrt(v + eps)

def _scatter_add(tgt, idx, src, axis=0):
    return tgt.at[idx].add(src)

def _segment_sum(src, seg, n):
    return jax.ops.segment_sum(src, seg, n)
kernel_name = 'mk_adj_preln_d4_adj_r2_b3a1ae'

def setup_inputs(seed: int=0):
    np.random.seed(seed)
    _w = jnp.asarray

    def _rec_inputs():
        import jax
        import jax.numpy as jnp
        _gk = jax.random.key(seed)
        x = -9.806e-05 + 1 * jax.random.normal(jax.random.fold_in(_gk, 1), (16, 512, 64), jnp.float32)
        _a = jax.random.bernoulli(jax.random.fold_in(_gk, 2), 0.03125, (16, 512, 512))
        _a = jnp.logical_or(_a, jnp.swapaxes(_a, -1, -2))
        _a = jnp.logical_or(_a, jnp.eye(512, dtype=bool))
        _af = _a.astype(jnp.float32)
        _af = _af * jax.random.uniform(jax.random.fold_in(_gk, 3), (16, 512, 512), jnp.float32, 0.05, 1)
        adj = _af
        return (x, adj)
    x, adj = _rec_inputs()

    def _L0_gnn_setup():
        import jax, jax.numpy as jnp
        import numpy as np
        K_ORDERS = 4

        def _cheb_forward(inputs, graph, weight, bias):
            B, N, C = inputs.shape
            eye = jnp.eye(N, dtype=graph.dtype)
            d = jnp.sum(graph, axis=-1) ** (-0.5)
            L = eye[None] - d[:, :, None] * graph * d[:, None, :]
            polys = [jnp.broadcast_to(eye, (B, N, N)), L]
            for _ in range(2, K_ORDERS):
                polys.append(2.0 * jnp.matmul(L, polys[-1]) - polys[-2])
            mul_L = jnp.stack(polys[:K_ORDERS], axis=0)
            prop = jnp.einsum('kbnm,bmc->kbnc', mul_L, inputs)
            out = jnp.einsum('kbnc,kcd->bnd', prop, weight[:, 0])
            return out + bias
        key = jax.random.key(seed)
        k1, k2, k3 = jax.random.split(key, 3)
        B, N, C, D = (8, 512, 64, 64)
        inputs = jax.random.normal(k1, (B, N, C), dtype=jnp.float32)
        graph = jax.random.uniform(k2, (B, N, N), dtype=jnp.float32)
        weight = jax.random.normal(k3, (K_ORDERS, 1, C, D), dtype=jnp.float32) * (2.0 / (C + D)) ** 0.5
        bias = jnp.zeros((1, 1, D), dtype=jnp.float32)
        return {'inputs': inputs, 'graph': graph, 'weight': weight, 'bias': bias}
    _L0_gnn_all = _L0_gnn_setup()
    _L0_gnn_in = {k: v for k, v in _L0_gnn_all.items() if k in ('weight', 'bias')}
    del _L0_gnn_all

    def _L1_gnn_setup():
        import jax, jax.numpy as jnp
        import numpy as np
        B, N, DIN, H, DOUT = (16, 1024, 64, 128, 64)
        NEG = 9000000000000000.0

        def _lin_params(key, fan_in, fan_out):
            kw, _ = jax.random.split(key)
            w = jax.random.normal(kw, (fan_in, fan_out), jnp.float32) / jnp.sqrt(float(fan_in))
            b = jnp.zeros((fan_out,), jnp.float32)
            return (w, b)

        def _att_layer(h, mask, wv, bv, wk, bk, wq, bq):
            v = jnp.tanh(h @ wv + bv)
            q = jnp.tanh(h @ wq + bq)
            k = jnp.tanh(h @ wk + bk)
            scores = jnp.einsum('bnd,bmd->bnm', q, k)
            att = jax.nn.softmax(scores * mask - NEG * (1.0 - mask), axis=2)
            return jnp.einsum('bnm,bmd->bnd', att, v)
        key = jax.random.key(seed)
        ks = jax.random.split(key, 16)
        x = jax.random.normal(ks[0], (B, N, DIN), jnp.float32)
        mask = jax.random.randint(ks[1], (B, N, N), 0, 2).astype(jnp.float32)
        enc_w, enc_b = _lin_params(ks[2], DIN, H)
        a1_wv, a1_bv = _lin_params(ks[3], H, H)
        a1_wk, a1_bk = _lin_params(ks[4], H, H)
        a1_wq, a1_bq = _lin_params(ks[5], H, H)
        a2_wv, a2_bv = _lin_params(ks[6], H, H)
        a2_wk, a2_bk = _lin_params(ks[7], H, H)
        a2_wq, a2_bq = _lin_params(ks[8], H, H)
        m_w1, m_b1 = _lin_params(ks[9], 2 * H, H)
        m_w2, m_b2 = _lin_params(ks[10], H, H)
        m_w3, m_b3 = _lin_params(ks[11], H, DOUT)
        return dict(x=x, mask=mask, enc_w=enc_w, enc_b=enc_b, a1_wv=a1_wv, a1_bv=a1_bv, a1_wk=a1_wk, a1_bk=a1_bk, a1_wq=a1_wq, a1_bq=a1_bq, a2_wv=a2_wv, a2_bv=a2_bv, a2_wk=a2_wk, a2_bk=a2_bk, a2_wq=a2_wq, a2_bq=a2_bq, m_w1=m_w1, m_b1=m_b1, m_w2=m_w2, m_b2=m_b2, m_w3=m_w3, m_b3=m_b3)
    _L1_gnn_all = _L1_gnn_setup()
    _L1_gnn_in = {k: v for k, v in _L1_gnn_all.items() if k in ('enc_w', 'enc_b', 'a1_wv', 'a1_bv', 'a1_wk', 'a1_bk', 'a1_wq', 'a1_bq', 'a2_wv', 'a2_bv', 'a2_wk', 'a2_bk', 'a2_wq', 'a2_bq', 'm_w1', 'm_b1', 'm_w2', 'm_b2', 'm_w3', 'm_b3')}
    del _L1_gnn_all

    def _L2_gnn_setup():
        import jax, jax.numpy as jnp
        import numpy as np
        B, N, F, U = (16, 1024, 64, 64)
        key = jax.random.key(seed)
        k1, k2, k3 = jax.random.split(key, 3)
        node_features = jax.random.normal(k1, (B, N, F), dtype=jnp.float32)
        adjacency_matrix = (jax.random.uniform(k2, (B, N, N)) < 0.01).astype(jnp.float32)
        kernel = jax.random.normal(k3, (F, U), dtype=jnp.float32) * (1.0 / np.sqrt(F))
        return {'node_features': node_features, 'adjacency_matrix': adjacency_matrix, 'kernel': kernel}
    _L2_gnn_all = _L2_gnn_setup()
    _L2_gnn_in = {k: v for k, v in _L2_gnn_all.items() if k in ('kernel',)}
    del _L2_gnn_all

    def _L3_gnn_setup():
        import jax, jax.numpy as jnp
        import numpy as np
        key = jax.random.key(seed)
        kx, ka = jax.random.split(key)
        B, N, F = (8, 1024, 64)
        x = jax.random.normal(kx, (B, N, F), dtype=jnp.float32)
        a = jax.random.uniform(ka, (B, N, N), dtype=jnp.float32)
        return {'x': x, 'a': a}
    _L3_gnn_all = _L3_gnn_setup()
    _L3_gnn_in = {k: v for k, v in _L3_gnn_all.items() if k in ()}
    del _L3_gnn_all
    return {'x': x, 'adj': adj, 'L0_gnn_weight': _L0_gnn_in['weight'], 'L0_gnn_bias': _L0_gnn_in['bias'], 'L1_gnn_enc_w': _L1_gnn_in['enc_w'], 'L1_gnn_enc_b': _L1_gnn_in['enc_b'], 'L1_gnn_a1_wv': _L1_gnn_in['a1_wv'], 'L1_gnn_a1_bv': _L1_gnn_in['a1_bv'], 'L1_gnn_a1_wk': _L1_gnn_in['a1_wk'], 'L1_gnn_a1_bk': _L1_gnn_in['a1_bk'], 'L1_gnn_a1_wq': _L1_gnn_in['a1_wq'], 'L1_gnn_a1_bq': _L1_gnn_in['a1_bq'], 'L1_gnn_a2_wv': _L1_gnn_in['a2_wv'], 'L1_gnn_a2_bv': _L1_gnn_in['a2_bv'], 'L1_gnn_a2_wk': _L1_gnn_in['a2_wk'], 'L1_gnn_a2_bk': _L1_gnn_in['a2_bk'], 'L1_gnn_a2_wq': _L1_gnn_in['a2_wq'], 'L1_gnn_a2_bq': _L1_gnn_in['a2_bq'], 'L1_gnn_m_w1': _L1_gnn_in['m_w1'], 'L1_gnn_m_b1': _L1_gnn_in['m_b1'], 'L1_gnn_m_w2': _L1_gnn_in['m_w2'], 'L1_gnn_m_b2': _L1_gnn_in['m_b2'], 'L1_gnn_m_w3': _L1_gnn_in['m_w3'], 'L1_gnn_m_b3': _L1_gnn_in['m_b3'], 'L2_gnn_kernel': _L2_gnn_in['kernel']}

def reference(x, adj, L0_gnn_weight, L0_gnn_bias, L1_gnn_enc_w, L1_gnn_enc_b, L1_gnn_a1_wv, L1_gnn_a1_bv, L1_gnn_a1_wk, L1_gnn_a1_bk, L1_gnn_a1_wq, L1_gnn_a1_bq, L1_gnn_a2_wv, L1_gnn_a2_bv, L1_gnn_a2_wk, L1_gnn_a2_bk, L1_gnn_a2_wq, L1_gnn_a2_bq, L1_gnn_m_w1, L1_gnn_m_b1, L1_gnn_m_w2, L1_gnn_m_b2, L1_gnn_m_w3, L1_gnn_m_b3, L2_gnn_kernel):
    import jax
    import jax.numpy as jnp

    def _L0_gnn_ref(inputs, graph, weight, bias):
        import jax, jax.numpy as jnp
        import numpy as np
        K_ORDERS = 4

        def _cheb_forward(inputs, graph, weight, bias):
            B, N, C = inputs.shape
            eye = jnp.eye(N, dtype=graph.dtype)
            d = jnp.sum(graph, axis=-1) ** (-0.5)
            L = eye[None] - d[:, :, None] * graph * d[:, None, :]
            polys = [jnp.broadcast_to(eye, (B, N, N)), L]
            for _ in range(2, K_ORDERS):
                polys.append(2.0 * jnp.matmul(L, polys[-1]) - polys[-2])
            mul_L = jnp.stack(polys[:K_ORDERS], axis=0)
            prop = jnp.einsum('kbnm,bmc->kbnc', mul_L, inputs)
            out = jnp.einsum('kbnc,kcd->bnd', prop, weight[:, 0])
            return out + bias
        return _cheb_forward(inputs, graph, weight, bias)

    def _L1_gnn_ref(x, mask, enc_w, enc_b, a1_wv, a1_bv, a1_wk, a1_bk, a1_wq, a1_bq, a2_wv, a2_bv, a2_wk, a2_bk, a2_wq, a2_bq, m_w1, m_b1, m_w2, m_b2, m_w3, m_b3):
        import jax, jax.numpy as jnp
        import numpy as np
        B, N, DIN, H, DOUT = (16, 1024, 64, 128, 64)
        NEG = 9000000000000000.0

        def _lin_params(key, fan_in, fan_out):
            kw, _ = jax.random.split(key)
            w = jax.random.normal(kw, (fan_in, fan_out), jnp.float32) / jnp.sqrt(float(fan_in))
            b = jnp.zeros((fan_out,), jnp.float32)
            return (w, b)

        def _att_layer(h, mask, wv, bv, wk, bk, wq, bq):
            v = jnp.tanh(h @ wv + bv)
            q = jnp.tanh(h @ wq + bq)
            k = jnp.tanh(h @ wk + bk)
            scores = jnp.einsum('bnd,bmd->bnm', q, k)
            att = jax.nn.softmax(scores * mask - NEG * (1.0 - mask), axis=2)
            return jnp.einsum('bnm,bmd->bnd', att, v)
        h1 = jnp.tanh(x @ enc_w + enc_b)
        h2 = _att_layer(h1, mask, a1_wv, a1_bv, a1_wk, a1_bk, a1_wq, a1_bq)
        h3 = _att_layer(h2, mask, a2_wv, a2_bv, a2_wk, a2_bk, a2_wq, a2_bq)
        h4 = jnp.concatenate([h2, h3], axis=2)
        z = jax.nn.relu(h4 @ m_w1 + m_b1)
        z = jax.nn.relu(z @ m_w2 + m_b2)
        return z @ m_w3 + m_b3

    def _L2_gnn_ref(node_features, adjacency_matrix, kernel):
        import jax, jax.numpy as jnp
        import numpy as np
        B, N, F, U = (16, 1024, 64, 64)
        n = adjacency_matrix.shape[-1]
        adj = adjacency_matrix + jnp.eye(n, dtype=adjacency_matrix.dtype)
        row_sum = jnp.sum(adj, axis=-1)
        d_inv_sqrt = jnp.where(row_sum > 0, row_sum ** (-0.5), 0.0)
        norm_adj = d_inv_sqrt[:, :, None] * adj * d_inv_sqrt[:, None, :]
        transformed = jnp.einsum('bnf,fu->bnu', node_features, kernel)
        out = jnp.einsum('bnm,bmu->bnu', norm_adj, transformed)
        return jax.nn.relu(out)

    def _L3_gnn_ref(x, a):
        import jax, jax.numpy as jnp
        import numpy as np
        t = jnp.einsum('bij,bjf->bif', a, x)
        out = jnp.where(t > 0.5, t / t, t * 0.0)
        return out
    h = jnp.maximum(_layernorm(x, axis=-1), 0.0)
    x = x + _L0_gnn_ref(h, adj, L0_gnn_weight, L0_gnn_bias)
    h = jnp.maximum(_layernorm(x, axis=-1), 0.0)
    x = x + _L1_gnn_ref(h, adj, L1_gnn_enc_w, L1_gnn_enc_b, L1_gnn_a1_wv, L1_gnn_a1_bv, L1_gnn_a1_wk, L1_gnn_a1_bk, L1_gnn_a1_wq, L1_gnn_a1_bq, L1_gnn_a2_wv, L1_gnn_a2_bv, L1_gnn_a2_wk, L1_gnn_a2_bk, L1_gnn_a2_wq, L1_gnn_a2_bq, L1_gnn_m_w1, L1_gnn_m_b1, L1_gnn_m_w2, L1_gnn_m_b2, L1_gnn_m_w3, L1_gnn_m_b3)
    h = jnp.maximum(_layernorm(x, axis=-1), 0.0)
    x = x + _L2_gnn_ref(h, adj, L2_gnn_kernel)
    h = jnp.maximum(_layernorm(x, axis=-1), 0.0)
    x = x + _L3_gnn_ref(h, adj)
    return x

_drawn_inputs = setup_inputs


def setup_inputs(seed=0):
    import zlib

    import numpy as np

    out = dict(_drawn_inputs(seed))
    spreads = {'L0_gnn_bias': (0.0, 0.1),
     'L1_gnn_enc_b': (0.0, 0.594),
     'L1_gnn_a1_bv': (0.0, 0.409),
     'L1_gnn_a1_bk': (0.0, 0.1),
     'L1_gnn_a1_bq': (0.0, 0.1),
     'L1_gnn_a2_bv': (0.0, 0.57),
     'L1_gnn_a2_bk': (0.0, 0.1),
     'L1_gnn_a2_bq': (0.0, 0.1),
     'L1_gnn_m_b1': (0.0, 0.413),
     'L1_gnn_m_b2': (0.0, 0.1),
     'L1_gnn_m_b3': (0.0, 0.1)}
    factors = {}
    for name, (base, spread) in spreads.items():
        noise = np.random.default_rng([zlib.crc32(name.encode()), seed]).standard_normal(out[name].shape)
        drawn = base * np.exp(spread * noise) if base else spread * noise
        out[name] = jnp.asarray(drawn.astype(out[name].dtype))
    for name, factor in factors.items():
        out[name] = (out[name] * factor).astype(out[name].dtype)
    return out
```

```python
from contextlib import ExitStack

import numpy as np

import concourse.bass as bass
from concourse import mybir

F32 = mybir.dt.float32
BF16 = mybir.dt.bfloat16
ALU = mybir.AluOpType
ACT = mybir.ActivationFunctionType

P = 128
SLOTS = 3
EPS = 1e-5
NEG = 9000000000000000.0
TINY = float(np.finfo(np.float32).tiny)

PRE = ["turn_a01", "turn_a23", "cheb_norm", "cheb_ht", "cheb_weights", "cheb_prop3", "cheb_prop2",
       "cheb_prop1", "enc_norm", "enc_ht", "encode"]
ATT = [(s, layer) for layer in range(2)
       for s in ("queries_keys", "values", "scores01", "turn0_scores2", "turn1_scores3", "turn2",
                 "turn3", "attend")]
POST = ["mlp1", "mlp2", "mlp3", "gcn_norm", "gcn_ht", "gcn_weights", "gcn_prop", "last_norm",
        "last_prop"]


def merged(*threads):
    keyed = [((k + 0.5) / len(steps), t, s) for t, steps in enumerate(threads)
             for k, s in enumerate(steps)]
    return [(t, s) for _, t, s in sorted(keyed, key=lambda x: x[:2])]


THREADS = ("att", "pre", "post")
ORDER = merged(ATT, PRE, POST)


class Graph:

    def __init__(self, turn, off):
        self.n = SLOTS * turn + off
        self.slot = off % SLOTS
        self.round = turn + off // SLOTS


class Chain:

    def __init__(self, sem, per_graph):
        self.sem, self.per, self.made = sem, per_graph, 0

    def begin(self, g):
        self.base, self.made = self.per * g.n, 0

    def add(self, ins):
        ins.then_inc(self.sem, 1)
        self.made += 1
        assert self.made <= self.per

    def so_far(self):
        return self.base + self.made

    def end(self):
        assert self.made == self.per, (self.made, self.per)


def graph_layers(nc, x, adj, cheb_w, cheb_b, enc_w, enc_b, att_w, att_b, w1, b1, w2, b2, w3, b3,
                 gcn_w, out):
    B, N, C = x.shape
    H = enc_w.shape[1]
    K = cheb_w.shape[0]
    RB = N // P
    assert H == P and K == 4 and RB == 4 and 2 * C == P and B % SLOTS == 1 and B >= 7

    x_d = x.rearrange("b (i p) c -> b p i c", p=P)
    adj_d = adj.rearrange("b (i p) m -> b p i m", p=P)
    out_d = out.rearrange("b (i p) c -> b p i c", p=P)

    with ExitStack() as ctx:
        def sb(name, shape, dt=F32):
            return ctx.enter_context(nc.sbuf_tensor(name, shape, dt))

        def sem(name):
            return ctx.enter_context(nc.semaphore(name))

        ident = sb("ident", [P, P])
        ones_bf = sb("ones_bf", [P, P], BF16)
        nhalf = sb("nhalf", [P, 2 * RB])
        cheb_ws = sb("cheb_ws", [C, K, C])
        enc_ws = sb("enc_ws", [C, H])
        att_ws = [[sb(f"att_w{a}{k}", [H, H]) for k in range(3)] for a in range(2)]
        w1_s = sb("w1_s", [H, 2, H])
        w2_s = sb("w2_s", [H, H])
        w3_s = sb("w3_s", [H, C])
        gcn_ws = sb("gcn_ws", [C, C])
        enc_bs = sb("enc_bs", [H, 1])
        kq_bs = [[None] + [sb(f"kq_b{a}{k}", [H, 1]) for k in (1, 2)] for a in range(2)]
        b1_s = sb("b1_s", [H, 1])
        b2_s = sb("b2_s", [H, 1])
        cheb_bs = sb("cheb_bs", [P, C])
        b3_s = sb("b3_s", [P, C])
        bv_f = [sb(f"bv_f{a}", [P, H]) for a in range(2)]
        bv_r = [sb(f"bv_r{a}", [P, H]) for a in range(2)]
        bv_rows = [sb(f"bv_rows{a}", [P, RB, H], BF16) for a in range(2)]

        a_nat = [sb(f"a_nat{s}", [P, RB, N]) for s in range(SLOTS)]
        a_t = [sb(f"a_t{s}", [P, RB, N]) for s in range(SLOTS)]
        gate = [sb(f"gate{s}", [P, RB, N]) for s in range(SLOTS)]
        x_in = [sb(f"x_in{s}", [P, RB, C]) for s in range(SLOTS)]
        x_b = sb("x_b", [P, RB, C])
        x1 = [sb(f"x1_{s}", [P, RB, C]) for s in range(SLOTS)]
        x1b = [sb(f"x1b_{s}", [P, RB, C]) for s in range(SLOTS)]
        rs = sb("rs", [P, 2 * RB])
        dinv = [sb(f"dinv{s}", [P, 2 * RB]) for s in range(SLOTS)]
        h1_t = [sb(f"h1_t{s}", [P, N]) for s in range(SLOTS)]
        h2_t = [sb(f"h2_t{s}", [P, N]) for s in range(SLOTS)]
        h3_t = [sb(f"h3_t{s}", [P, N]) for s in range(SLOTS)]
        x_out = [sb(f"x_out{s}", [P, RB, C]) for s in range(SLOTS)]

        junk = sb("junk", [P, N])
        positive = sb("positive", [P, RB])
        d_m2 = sb("d_m2", [P, RB])
        d_neg = sb("d_neg", [P, RB])
        d_root = sb("d_root", [P, RB])
        stats = {t: sb(f"stats_{t}", [P, RB, 6]) for t in ("pre", "post")}
        meanvar = {t: sb(f"meanvar_{t}", [P, RB, 2]) for t in ("pre", "post")}
        vareps = {t: sb(f"vareps_{t}", [P, RB]) for t in ("pre", "post")}
        rstd = {t: sb(f"rstd_{t}", [P, RB]) for t in ("pre", "post")}
        centred = {t: sb(f"centred_{t}", [P, RB, C]) for t in ("pre", "post")}
        h_nat = {t: sb(f"h_nat_{t}", [P, RB, C]) for t in ("pre", "post")}
        h_t = {t: sb(f"h_t_{t}", [C, N]) for t in ("pre", "post")}
        c3 = sb("c3", [P, RB, C])
        c2 = sb("c2", [P, RB, C])
        c1 = sb("c1", [P, RB, C])
        e2 = sb("e2", [P, RB, C])
        e1 = sb("e1", [P, RB, C])
        f0 = sb("f0", [P, RB, C])
        tmp = sb("tmp", [P, RB, C])
        q_t = sb("q_t", [P, N])
        k_t = sb("k_t", [P, N])
        v_n = sb("v_n", [P, RB, H])
        negz = sb("negz", [P, RB, N])
        negmax = sb("negmax", [P, RB])
        probs = sb("probs", [P, RB, N])
        total = sb("total", [P, RB])
        inv_total = sb("inv_total", [P, RB])
        probs_t = sb("probs_t", [P, RB, N])
        inv_row = sb("inv_row", [P, N])
        z1_t = sb("z1_t", [P, N])
        z2_t = sb("z2_t", [P, N])
        x2 = sb("x2", [P, RB, C])
        x3 = sb("x3", [P, RB, C])
        u2 = sb("u2", [P, RB, C])
        s2 = sb("s2", [P, RB, C])
        last = sb("last", [P, RB, C])

        att_ps = [ctx.enter_context(nc.psum_tensor(f"att_ps{k}", [P, N], F32)) for k in range(4)]
        pre_ps = ctx.enter_context(nc.psum_tensor("pre_ps", [P, 2, N], F32))
        post_ps = [ctx.enter_context(nc.psum_tensor(f"post_ps{k}", [P, N], F32)) for k in range(2)]

        weights_in = sem("weights_in")
        consts_done = sem("consts_done")
        bias_rows = sem("bias_rows")
        a_loaded = [sem(f"a_loaded{s}") for s in range(SLOTS)]
        x_loaded = [sem(f"x_loaded{s}") for s in range(SLOTS)]
        out_sent = [sem(f"out_sent{s}") for s in range(SLOTS)]
        at_ready = sem("at_ready")
        ht_ready = {t: sem(f"ht_ready_{t}") for t in ("pre", "post")}
        cheb_ready = sem("cheb_ready")
        prop_ready = sem("prop_ready")
        enc_ready = sem("enc_ready")
        qk_ready = sem("qk_ready")
        v_ready = sem("v_ready")
        scores_ready = sem("scores_ready")
        pt_ready = sem("pt_ready")
        inv_ready = sem("inv_ready")
        pv_ready = sem("pv_ready")
        mlp_ready = sem("mlp_ready")
        gcn_ready = sem("gcn_ready")
        last_ready = sem("last_ready")
        rowsums = sem("rowsums")
        at_copied = sem("at_copied")
        ht_copied = {t: sem(f"ht_copied_{t}") for t in ("pre", "post")}
        h1_done = sem("h1_done")
        qk_done = sem("qk_done")
        v_done = sem("v_done")
        probs_done = sem("probs_done")
        pt_copied = sem("pt_copied")
        inv_copied = sem("inv_copied")
        z_done = sem("z_done")
        var_ready = {t: sem(f"var_ready_{t}") for t in ("pre", "post")}
        h_ready = {t: sem(f"h_ready_{t}") for t in ("pre", "post")}
        cheb_taken = sem("cheb_taken")
        c_ready = sem("c_ready")
        x1_done = sem("x1_done")
        masked = sem("masked")
        biased = sem("biased")
        inv_done = sem("inv_done")
        attended = sem("attended")
        x2_done = sem("x2_done")
        u2_done = sem("u2_done")
        x3_done = sem("x3_done")
        out_done = sem("out_done")
        dve_pre = Chain(sem("dve_pre"), 2 * 6 + 9)
        dve_post = Chain(sem("dve_post"), 2 * 6 + 3)
        gate_done = sem("gate_done")
        xb_done = sem("xb_done")
        x1b_done = sem("x1b_done")
        dinv_done = sem("dinv_done")
        rstd_done = {t: sem(f"rstd_done_{t}") for t in ("pre", "post")}
        pool_pre = Chain(sem("pool_pre"), 7)

        def over_blocks(per_row):
            return per_row.unsqueeze(2).to_broadcast([P, RB, C])

        def over_rows(per_channel):
            return per_channel.unsqueeze(1).to_broadcast([P, RB, C])

        def rows(ps):
            return ps[:, 0:RB * C].rearrange("p (i c) -> p i c", c=C)

        def cheb_part(k):
            return pre_ps[:, :, :].rearrange("p a (i k c) -> p (a i) k c", i=RB // 2, c=C)[:, :, k, :]

        def walk(eng_steps, begin=None):
            def one(g_pre, g_att, g_post):
                graphs = {"pre": g_pre, "att": g_att, "post": g_post}
                for t, g in graphs.items():
                    if g is not None and begin and t in begin:
                        begin[t].begin(g)
                for t, s in ORDER:
                    g = graphs[THREADS[t]]
                    if g is None:
                        continue
                    name, args = s if isinstance(s, tuple) else (s, None)
                    if name in eng_steps:
                        if args is None:
                            eng_steps[name](g)
                        else:
                            eng_steps[name](g, args)
                for t, g in graphs.items():
                    if g is not None and begin and t in begin:
                        begin[t].end()
            return one

        def rounds(eng, one):
            one(Graph(0, 0), None, None)
            one(Graph(0, 1), Graph(0, 0), None)
            one(Graph(0, 2), Graph(0, 1), Graph(0, 0))
            with eng.Fori(0, (B - 4) // SLOTS) as turn:
                for u in range(2, 2 + SLOTS):
                    one(Graph(turn, u + 1), Graph(turn, u), Graph(turn, u - 1))
            one(Graph(0, B - 1), Graph(0, B - 2), Graph(0, B - 3))
            one(None, Graph(0, B - 1), Graph(0, B - 2))
            one(None, None, Graph(0, B - 1))

        held = sem("held")

        def hold(eng):
            eng.sem_inc(held)

        block = ctx.enter_context(nc.Block())

        @block.sync
        def _(sp):
            small = [(cheb_ws[:], cheb_w.rearrange("k o c d -> (o c) k d")),
                     (enc_ws[:], enc_w), (w1_s[:], w1.rearrange("(a h) n -> h a n", a=2)),
                     (w2_s[:], w2), (w3_s[:], w3), (gcn_ws[:], gcn_w),
                     (enc_bs[:], enc_b.rearrange("(h o) -> h o", o=1)),
                     (b1_s[:], b1.rearrange("(h o) -> h o", o=1)),
                     (b2_s[:], b2.rearrange("(h o) -> h o", o=1)),
                     (cheb_bs[:], cheb_b.rearrange("a b c -> (a b c)").partition_broadcast(P)),
                     (b3_s[:], b3.partition_broadcast(P))]
            for a in range(2):
                small += [(att_ws[a][k][:], att_w[a][k]) for k in range(3)]
                small += [(kq_bs[a][k][:], att_b[a][k].rearrange("(h o) -> h o", o=1)) for k in (1, 2)]
                small += [(bv_f[a][:], att_b[a][0].partition_broadcast(P))]

            def load(g, waits=True):
                if waits:
                    sp.wait_ge(biased, 8 * (g.n - SLOTS) + 8)
                    hold(sp)
                    sp.wait_ge(x1_done, g.n - SLOTS + 1)
                sp.dma_start(x_in[g.slot][:], x_d[g.n]).then_inc(x_loaded[g.slot], 16)
                sp.dma_start(a_nat[g.slot][:], adj_d[g.n]).then_inc(a_loaded[g.slot], 16)

            def store(g):
                sp.wait_ge(out_done, g.n + 1)
                sp.dma_start(out_d[g.n], x_out[g.slot][:]).then_inc(out_sent[g.slot], 16)

            load(Graph(0, 0), False)
            for to, what in small:
                sp.dma_start(to, what).then_inc(weights_in, 16)
            load(Graph(0, 1), False)
            load(Graph(0, 2), False)
            load(Graph(0, 3))
            store(Graph(0, 0))
            with sp.Fori(0, (B - 4) // SLOTS) as turn:
                for u in range(2, 2 + SLOTS):
                    load(Graph(turn, u + 2))
                    store(Graph(turn, u - 1))
            for n in range(B - 3, B):
                store(Graph(0, n))
            for s in range(SLOTS):
                sp.wait_ge(out_sent[s], 16 * len(range(s, B, SLOTS)))

        n_small = 11 + 2 * 6
        n_bias_rows = 2 * (3 + 2 + 1 + 2 + 1 + RB - 1)

        @block.gpsimd
        def _(pool):
            gp = nc.gpsimd
            gp.memset(ident[:], 0.0).then_inc(consts_done, 1)
            gp.memset(ones_bf[:], 1.0).then_inc(consts_done, 1)
            gp.memset(nhalf[:], -0.5).then_inc(consts_done, 1)
            for a in range(2):
                gp.memset(bv_rows[a][:], 0.0).then_inc(consts_done, 1)
            pool.wait_ge(consts_done, 5)
            gp.affine_select(out=ident[:], in_=ident[:], compare_op=ALU.not_equal, fill=1.0, base=0,
                             pattern=[[-1, P]], channel_multiplier=1).then_inc(consts_done, 1)
            pool.wait_ge(weights_in, 16 * n_small)

            def scale_norm(t, k):
                def f(g):
                    pool.wait_ge(var_ready[t], 2 * g.n + k + 1)
                    gp.tensor_tensor(rstd[t][:], vareps[t][:], nhalf[:, 0:RB], ALU.pow)\
                        .then_inc(rstd_done[t], 1)
                return f

            def cheb_norm(g):
                scale_norm("pre", 0)(g)
                pool.wait_ge(x_loaded[g.slot], 16 * (g.round + 1))
                if not isinstance(g.n, int) or g.n > 0:
                    pool.wait_ge(x1_done, g.n)
                gp.tensor_tensor(x_b[:], x_in[g.slot][:], over_rows(cheb_bs[:]), ALU.add)\
                    .then_inc(xb_done, 1)
                pool.wait_ge(rowsums, 4 * g.n + 4)
                hold(pool)
                d = dinv[g.slot]
                pool_pre.add(gp.tensor_scalar(rs[:, RB:], rs[:, 0:RB], 1.0, TINY, ALU.add, ALU.max))
                pool_pre.add(gp.tensor_scalar(positive[:], rs[:, 0:RB], 1.0, 0.0, ALU.add, ALU.is_gt))
                pool.wait_ge(pool_pre.sem, pool_pre.so_far())
                pool_pre.add(gp.tensor_tensor(d[:], rs[:], nhalf[:], ALU.pow))
                pool.wait_ge(pool_pre.sem, pool_pre.so_far())
                pool_pre.add(gp.tensor_tensor(d[:, RB:], d[:, RB:], positive[:], ALU.mult))
                pool_pre.add(gp.tensor_scalar(d_neg[:], d[:, 0:RB], -1.0, None, ALU.mult))
                pool_pre.add(gp.tensor_tensor(d_root[:], d[:, 0:RB], rs[:, 0:RB], ALU.mult))
                pool_pre.add(gp.tensor_scalar(d_m2[:], d[:, 0:RB], -2.0, None, ALU.mult))
                pool.wait_ge(pool_pre.sem, pool_pre.so_far())
                gp.tensor_tensor(d_m2[:], d_m2[:], d[:, 0:RB], ALU.mult).then_inc(dinv_done, 1)

            def turn_a01(g):
                pool.wait_ge(a_loaded[g.slot], 16 * (g.round + 1))
                hold(pool)
                gp.tensor_scalar(gate[g.slot][:], a_nat[g.slot][:], 1.0, NEG, ALU.subtract, ALU.mult)\
                    .then_inc(gate_done, 1)

            def enc_norm(g):
                scale_norm("pre", 1)(g)
                pool.wait_ge(x1_done, g.n + 1)
                gp.tensor_tensor(x1b[g.slot][:], x1[g.slot][:], over_rows(b3_s[:]), ALU.add)\
                    .then_inc(x1b_done, 1)

            steps = {"cheb_norm": cheb_norm, "turn_a23": turn_a01, "enc_norm": enc_norm,
                     "gcn_norm": scale_norm("post", 0), "last_norm": scale_norm("post", 1)}
            rounds(pool, walk(steps, {"pre": pool_pre}))

        @block.scalar
        def _(act):
            sc = nc.scalar
            act.wait_ge(weights_in, 16 * n_small)

            def copy_at(g, js):
                for j in js:
                    act.wait_ge(at_ready, 4 * g.n + j + 1)
                    sc.activation(a_t[g.slot][:, j, :], pre_ps[:, j % 2, :], ACT.Copy)\
                        .then_inc(at_copied, 1)

            def turn_a01(g):
                act.wait_ge(a_loaded[g.slot], 16 * (g.round + 1))
                if not isinstance(g.n, int) or g.n > 0:
                    act.wait_ge(dinv_done, g.n)
                    act.wait_ge(rowsums, 4 * g.n)
                for i in range(RB):
                    if i:
                        act.wait_ge(rowsums, 4 * g.n + i)
                    sc.activation(junk[:], a_nat[g.slot][:, i, :], ACT.Copy,
                                  accum_out=rs[:, i:i + 1]).then_inc(rowsums, 1)
                copy_at(g, (0, 1))

            def copy_ht(t, k, per, ps):
                def f(g):
                    act.wait_ge(ht_ready[t], per * g.n + k + 1)
                    sc.activation(h_t[t][:], ps, ACT.Copy).then_inc(ht_copied[t], 1)
                return f

            def encode(g):
                act.wait_ge(enc_ready, g.n + 1)
                sc.activation(h1_t[g.slot][:], pre_ps[:, 0, :], ACT.Tanh, bias=enc_bs[:])\
                    .then_inc(h1_done, 1)

            def queries_keys(g, a):
                for k, (to, which) in enumerate(((q_t, 2), (k_t, 1))):
                    act.wait_ge(qk_ready, 4 * g.n + 2 * a + k + 1)
                    sc.activation(to[:], att_ps[k][:], ACT.Tanh, bias=kq_bs[a][which][:])\
                        .then_inc(qk_done, 1)

            def values(g, a):
                act.wait_ge(v_ready, 2 * g.n + a + 1)
                sc.activation(v_n[:].rearrange("p i h -> p (i h)"), att_ps[2][:], ACT.Tanh)\
                    .then_inc(v_done, 1)

            def exponent(g, a, i):
                act.wait_ge(biased, 8 * g.n + 4 * a + i + 1)
                sc.activation(probs[:, i, :], negz[:, i, :], ACT.Exp, bias=negmax[:, i:i + 1],
                              scale=-1.0, accum_out=total[:, i:i + 1]).then_inc(probs_done, 1)

            def copy_pt(g, a, i):
                act.wait_ge(pt_ready, 8 * g.n + 4 * a + i + 1)
                sc.activation(probs_t[:, :, i * P:(i + 1) * P],
                              att_ps[2 + i % 2][:].rearrange("p (j n) -> p j n", n=P), ACT.Copy)\
                    .then_inc(pt_copied, 1)

            def scores01(g, a):
                exponent(g, a, 0)

            def turn0_scores2(g, a):
                exponent(g, a, 1)
                copy_pt(g, a, 0)

            def turn1_scores3(g, a):
                exponent(g, a, 2)
                copy_pt(g, a, 1)

            def turn2(g, a):
                exponent(g, a, 3)
                copy_pt(g, a, 2)

            def turn3(g, a):
                copy_pt(g, a, 3)
                act.wait_ge(inv_ready, 2 * g.n + a + 1)
                sc.activation(inv_row[:], att_ps[1][:], ACT.Copy).then_inc(inv_copied, 1)

            def mlp(k, to, ps, bias):
                def f(g):
                    act.wait_ge(mlp_ready, 3 * g.n + k + 1)
                    sc.activation(to[:], ps[:], ACT.Relu, bias=bias[:]).then_inc(z_done, 1)
                return f

            steps = {"turn_a01": turn_a01, "turn_a23": lambda g: copy_at(g, (2, 3)),
                     "cheb_ht": copy_ht("pre", 0, 2, pre_ps[0:C, 0, :]),
                     "enc_ht": copy_ht("pre", 1, 2, pre_ps[0:C, 1, :]),
                     "encode": encode, "queries_keys": queries_keys, "values": values,
                     "scores01": scores01, "turn0_scores2": turn0_scores2,
                     "turn1_scores3": turn1_scores3, "turn2": turn2, "turn3": turn3,
                     "mlp1": mlp(0, z1_t, post_ps[0], b1_s), "mlp2": mlp(1, z2_t, post_ps[1], b2_s),
                     "gcn_ht": copy_ht("post", 0, 1, post_ps[1][0:C, :])}
            rounds(act, walk(steps))

        @block.vector
        def _(dve):
            ve = nc.vector

            dve.wait_ge(weights_in, 16 * n_small)
            dve.wait_ge(consts_done, 6)
            made = 0
            for a in range(2):
                rest = bv_f[a]
                for row, p0 in enumerate((0, 32, 64)):
                    for p1 in range(p0, 96, 32):
                        ve.tensor_copy(bv_rows[a][p1:p1 + 1, 0, :], rest[p1:p1 + 1, :])\
                            .then_inc(bias_rows, 1)
                        made += 1
                    dve.wait_ge(bias_rows, made)
                    for p1 in range(p0 + 32, 96, 32):
                        ve.tensor_tensor(rest[p1:p1 + 1, :], rest[p1:p1 + 1, :],
                                         bv_rows[a][p1:p1 + 1, 0, :], ALU.subtract)\
                            .then_inc(bias_rows, 1)
                        made += 1
                    dve.wait_ge(bias_rows, made)
                for i in range(1, RB):
                    ve.tensor_copy(bv_rows[a][0:96, i, :], bv_rows[a][0:96, 0, :])\
                        .then_inc(bias_rows, 1)
                    made += 1
            assert made == n_bias_rows

            def norm_stats(t, chain, g, k, src):
                st, mv = stats[t], meanvar[t]
                for i in range(RB):
                    chain.add(ve.bn_stats(st[:, i, :], src[:, i, :]))
                dve.wait_ge(chain.sem, chain.so_far())
                hold(dve)
                for i in range(RB):
                    last_one = ve.bn_aggr(mv[:, i, :], st[:, i, :])
                chain.add(last_one)
                dve.wait_ge(chain.sem, chain.so_far())
                ve.tensor_scalar(vareps[t][:], mv[:, :, 1], EPS, None, ALU.add)\
                    .then_inc(var_ready[t], 1)
                chain.add(ve.tensor_tensor(centred[t][:], src[:], mv[:, :, 0:1].to_broadcast([P, RB, C]),
                                           ALU.subtract))

            def norm_apply(t, chain, g, k):
                dve.wait_ge(rstd_done[t], 2 * g.n + k + 1)
                dve.wait_ge(chain.sem, chain.so_far())
                ve.scalar_tensor_tensor(h_nat[t][:], centred[t][:], 0.0, over_blocks(rstd[t][:]),
                                        ALU.max, ALU.mult).then_inc(h_ready[t], 1)

            def turn_a01(g):
                dve.wait_ge(x_loaded[g.slot], 16 * (g.round + 1))
                norm_stats("pre", dve_pre, g, 0, x_in[g.slot])

            def cheb_norm(g):
                if not isinstance(g.n, int) or g.n > 0:
                    dve.wait_ge(ht_ready["pre"], 2 * g.n)
                norm_apply("pre", dve_pre, g, 0)

            def cheb_weights(g):
                d = over_blocks(dinv[g.slot][:, 0:RB])
                dve.wait_ge(cheb_ready, g.n + 1)
                dve.wait_ge(dinv_done, g.n + 1)
                ve.tensor_tensor(c3[:], cheb_part(3), d, ALU.mult).then_inc(cheb_taken, 1)
                ve.tensor_tensor(e2[:], cheb_part(2), d, ALU.mult).then_inc(cheb_taken, 1)
                ve.tensor_tensor(e1[:], cheb_part(1), d, ALU.mult).then_inc(cheb_taken, 1)
                dve.wait_ge(xb_done, g.n + 1)
                ve.tensor_tensor(f0[:], cheb_part(0), x_b[:], ALU.add).then_inc(cheb_taken, 1)
                dve.wait_ge(cheb_taken, 4 * g.n + 3)
                dve_pre.add(ve.scalar_tensor_tensor(e2[:], c3[:], 2.0, e2[:], ALU.mult, ALU.add))
                dve_pre.add(ve.tensor_tensor(e1[:], e1[:], c3[:], ALU.subtract))

            def cheb_prop3(g):
                dve.wait_ge(prop_ready, 3 * g.n + 1)
                dve_pre.add(ve.tensor_tensor(tmp[:], rows(pre_ps[:, 0, :]), over_blocks(d_m2[:]), ALU.mult))
                dve.wait_ge(dve_pre.sem, dve_pre.so_far())
                ve.tensor_tensor(c2[:], tmp[:], e2[:], ALU.add).then_inc(c_ready, 1)
                dve.wait_ge(c_ready, 2 * g.n + 1)
                dve_pre.add(ve.scalar_tensor_tensor(e1[:], c2[:], 2.0, e1[:], ALU.mult, ALU.add))

            def cheb_prop2(g):
                dve.wait_ge(prop_ready, 3 * g.n + 2)
                dve_pre.add(ve.tensor_tensor(tmp[:], rows(pre_ps[:, 1, :]), over_blocks(d_m2[:]), ALU.mult))
                dve.wait_ge(dve_pre.sem, dve_pre.so_far())
                ve.tensor_tensor(c1[:], tmp[:], e1[:], ALU.add).then_inc(c_ready, 1)
                dve.wait_ge(c_ready, 2 * g.n + 2)
                dve_pre.add(ve.tensor_tensor(tmp[:], c1[:], c2[:], ALU.subtract))
                dve.wait_ge(dve_pre.sem, dve_pre.so_far())
                dve_pre.add(ve.tensor_tensor(tmp[:], tmp[:], over_blocks(d_root[:]), ALU.mult))
                dve.wait_ge(dve_pre.sem, dve_pre.so_far())
                dve.wait_ge(cheb_taken, 4 * g.n + 4)
                dve_pre.add(ve.tensor_tensor(f0[:], f0[:], tmp[:], ALU.add))

            def cheb_prop1(g):
                dve.wait_ge(prop_ready, 3 * g.n + 3)
                dve.wait_ge(dve_pre.sem, dve_pre.so_far())
                dve_pre.add(ve.tensor_tensor(tmp[:], rows(pre_ps[:, 0, :]), over_blocks(d_neg[:]), ALU.mult))
                dve.wait_ge(dve_pre.sem, dve_pre.so_far())
                ve.tensor_tensor(x1[g.slot][:], tmp[:], f0[:], ALU.add).then_inc(x1_done, 1)
                dve.wait_ge(x1_done, g.n + 1)
                norm_stats("pre", dve_pre, g, 1, x1[g.slot])

            def enc_norm(g):
                norm_apply("pre", dve_pre, g, 1)

            def mask(g, a, i):
                n = 4 * a + i
                s = g.slot
                dve.wait_ge(scores_ready, 8 * g.n + n + 1)
                ve.tensor_tensor(negz[:, i, :], att_ps[i % 2][:], a_nat[s][:, i, :], ALU.mult)\
                    .then_inc(masked, 1)
                if n == 0:
                    dve.wait_ge(gate_done, g.n + 1)
                dve.wait_ge(masked, 8 * g.n + n + 1)
                hold(dve)
                ve.tensor_tensor_reduce(negz[:, i, :], negz[:, i, :], gate[s][:, i, :], -1.0, 3.0e38,
                                        ALU.add, ALU.min, negmax[:, i:i + 1]).then_inc(biased, 1)

            def scores01(g, a):
                mask(g, a, 0)
                mask(g, a, 1)

            def turn0_scores2(g, a):
                mask(g, a, 2)

            def turn1_scores3(g, a):
                mask(g, a, 3)

            def turn3(g, a):
                dve.wait_ge(probs_done, 8 * g.n + 4 * a + 4)
                ve.reciprocal(inv_total[:], total[:]).then_inc(inv_done, 1)

            def attend(g, a):
                to = (h2_t, h3_t)[a][g.slot]
                dve.wait_ge(inv_copied, 2 * g.n + a + 1)
                dve.wait_ge(pv_ready, 2 * g.n + a + 1)
                ve.tensor_tensor(to[:], att_ps[0][:], inv_row[:], ALU.mult).then_inc(attended, 1)

            def mlp3(g):
                dve.wait_ge(mlp_ready, 3 * g.n + 3)
                dve.wait_ge(x1b_done, g.n + 1)
                ve.tensor_tensor(x2[:], rows(post_ps[0][:]), x1b[g.slot][:], ALU.add).then_inc(x2_done, 1)
                dve.wait_ge(x2_done, g.n + 1)
                norm_stats("post", dve_post, g, 0, x2)

            def gcn_norm(g):
                norm_apply("post", dve_post, g, 0)

            def gcn_weights(g):
                dve.wait_ge(gcn_ready, 2 * g.n + 1)
                ve.tensor_tensor(u2[:], rows(post_ps[0][:]), over_blocks(dinv[g.slot][:, RB:]), ALU.mult)\
                    .then_inc(u2_done, 1)

            def gcn_prop(g):
                dve.wait_ge(gcn_ready, 2 * g.n + 2)
                dve.wait_ge(u2_done, g.n + 1)
                dve_post.add(ve.tensor_tensor(s2[:], rows(post_ps[1][:]), u2[:], ALU.add))
                dve.wait_ge(dve_post.sem, dve_post.so_far())
                dve_post.add(ve.tensor_tensor(s2[:], s2[:], over_blocks(dinv[g.slot][:, RB:]), ALU.mult))
                dve.wait_ge(dve_post.sem, dve_post.so_far())
                ve.scalar_tensor_tensor(x3[:], s2[:], 0.0, x2[:], ALU.max, ALU.add).then_inc(x3_done, 1)
                dve.wait_ge(x3_done, g.n + 1)
                norm_stats("post", dve_post, g, 1, x3)

            def last_norm(g):
                norm_apply("post", dve_post, g, 1)

            def last_prop(g):
                dve.wait_ge(last_ready, g.n + 1)
                dve_post.add(ve.scalar_tensor_tensor(last[:], rows(post_ps[0][:]), 0.5, x3[:],
                                                     ALU.is_gt, ALU.add))
                dve.wait_ge(dve_post.sem, dve_post.so_far())
                if not isinstance(g.n, int) or g.n >= SLOTS:
                    dve.wait_ge(out_sent[g.slot], 16 * g.round)
                ve.scalar_tensor_tensor(x_out[g.slot][:], rows(post_ps[0][:]), 0.0, last[:],
                                        ALU.mult, ALU.add).then_inc(out_done, 1)

            steps = {"turn_a01": turn_a01, "cheb_norm": cheb_norm, "cheb_weights": cheb_weights,
                     "cheb_prop3": cheb_prop3, "cheb_prop2": cheb_prop2, "cheb_prop1": cheb_prop1,
                     "enc_norm": enc_norm, "scores01": scores01, "turn0_scores2": turn0_scores2,
                     "turn1_scores3": turn1_scores3, "turn3": turn3, "attend": attend,
                     "mlp3": mlp3, "gcn_norm": gcn_norm, "gcn_weights": gcn_weights,
                     "gcn_prop": gcn_prop, "last_norm": last_norm, "last_prop": last_prop}
            rounds(dve, walk(steps, {"pre": dve_pre, "post": dve_post}))

        @block.tensor
        def _(pe):
            te = nc.tensor
            pe.wait_ge(consts_done, 6)
            pe.wait_ge(weights_in, 16 * n_small)
            pe.wait_ge(bias_rows, n_bias_rows)

            def turn_a(g, js):
                pe.wait_ge(a_loaded[g.slot], 16 * (g.round + 1))
                for j in js:
                    if j < 2:
                        if j == 0 and (not isinstance(g.n, int) or g.n > 0):
                            pe.wait_ge(h1_done, g.n)
                    else:
                        pe.wait_ge(at_copied, 4 * g.n + j - 1)
                    for i in range(RB):
                        mm = te.transpose(pre_ps[:, j % 2, i * P:(i + 1) * P],
                                          a_nat[g.slot][:, i, j * P:(j + 1) * P], ident[:])
                    mm.then_inc(at_ready, 1)

            def turn_h(t, ready, g, bank):
                pe.wait_ge(h_ready[t], ready)
                hold(pe)
                for i in range(RB):
                    mm = te.transpose(bank[0:C, i * P:(i + 1) * P], h_nat[t][:, i, :], ident[:])
                mm.then_inc(ht_ready[t], 1)

            def cheb_ht(g):
                pe.wait_ge(at_copied, 4 * g.n + 3)
                turn_h("pre", 2 * g.n + 1, g, pre_ps[:, 0, :])

            def cheb_weights(g):
                pe.wait_ge(at_copied, 4 * g.n + 4)
                pe.wait_ge(ht_copied["pre"], 2 * g.n + 1)
                for i in range(RB):
                    w = K * C
                    mm = te.matmul(pre_ps[:, i // 2, i % 2 * w:(i % 2 + 1) * w],
                                   h_t["pre"][:, i * P:(i + 1) * P],
                                   cheb_ws[:].rearrange("c k d -> c (k d)"), start=True, stop=True)
                mm.then_inc(cheb_ready, 1)

            def propagate(g, bank, u):
                for i in range(RB):
                    for j in range(RB):
                        mm = te.matmul(bank[:, i * C:(i + 1) * C],
                                       a_t[g.slot][:, j, i * P:(i + 1) * P], u[:, j, :],
                                       start=(j == 0), stop=(j == RB - 1))
                return mm

            def cheb_prop3(g):
                pe.wait_ge(cheb_taken, 4 * g.n + 4)
                propagate(g, pre_ps[:, 0, :], c3).then_inc(prop_ready, 1)

            def cheb_prop2(g):
                pe.wait_ge(c_ready, 2 * g.n + 1)
                propagate(g, pre_ps[:, 1, :], c2).then_inc(prop_ready, 1)

            def cheb_prop1(g):
                pe.wait_ge(c_ready, 2 * g.n + 2)
                propagate(g, pre_ps[:, 0, :], c1).then_inc(prop_ready, 1)

            def enc_ht(g):
                turn_h("pre", 2 * g.n + 2, g, pre_ps[:, 1, :])

            def encode(g):
                pe.wait_ge(ht_copied["pre"], 2 * g.n + 2)
                te.matmul(pre_ps[:, 0, :], enc_ws[:], h_t["pre"][:], start=True, stop=True)\
                    .then_inc(enc_ready, 1)

            def source(g, a):
                return (h1_t, h2_t)[a][g.slot]

            def queries_keys(g, a):
                if a == 0:
                    pe.wait_ge(h1_done, g.n + 1)
                    if not isinstance(g.n, int) or g.n > 0:
                        pe.wait_ge(attended, 2 * g.n)
                else:
                    pe.wait_ge(attended, 2 * g.n + 1)
                for k, which in enumerate((2, 1)):
                    te.matmul(att_ps[k][:], att_ws[a][which][:], source(g, a)[:],
                              start=True, stop=True).then_inc(qk_ready, 1)

            def values(g, a):
                te.matmul(att_ps[2][:], ones_bf[:, :],
                          bv_rows[a][:].rearrange("p i h -> p (i h)"), start=True, stop=False,
                          skip_group_check=True)
                for i in range(RB):
                    mm = te.matmul(att_ps[2][:, i * P:(i + 1) * P],
                                   source(g, a)[:, i * P:(i + 1) * P], att_ws[a][0][:],
                                   start=False, stop=(i == RB - 1), skip_group_check=True)
                mm.then_inc(v_ready, 1)

            def scores(g, a, i):
                if i < 2:
                    pe.wait_ge(qk_done, 4 * g.n + 2 * a + 2)
                else:
                    pe.wait_ge(masked, 8 * g.n + 4 * a + i - 1)
                te.matmul(att_ps[i % 2][:], q_t[:, i * P:(i + 1) * P], k_t[:], start=True, stop=True)\
                    .then_inc(scores_ready, 1)

            def turn_probs(g, a, i):
                pe.wait_ge(probs_done, 8 * g.n + 4 * a + i + 1)
                if i == 0:
                    pe.wait_ge(v_done, 2 * g.n + a + 1)
                if i >= 2:
                    pe.wait_ge(pt_copied, 8 * g.n + 4 * a + i - 1)
                for j in range(RB):
                    mm = te.transpose(att_ps[2 + i % 2][:, j * P:(j + 1) * P],
                                      probs[:, i, j * P:(j + 1) * P], ident[:])
                mm.then_inc(pt_ready, 1)

            def scores01(g, a):
                scores(g, a, 0)
                scores(g, a, 1)

            def turn0_scores2(g, a):
                scores(g, a, 2)
                turn_probs(g, a, 0)

            def turn1_scores3(g, a):
                scores(g, a, 3)
                turn_probs(g, a, 1)

            def turn2(g, a):
                turn_probs(g, a, 2)

            def turn3(g, a):
                turn_probs(g, a, 3)
                pe.wait_ge(inv_done, 2 * g.n + a + 1)
                for i in range(RB):
                    mm = te.transpose(att_ps[1][:, i * P:(i + 1) * P],
                                      inv_total[:, i:i + 1].to_broadcast([P, P]), ident[:])
                mm.then_inc(inv_ready, 1)

            def attend(g, a):
                pe.wait_ge(pt_copied, 8 * g.n + 4 * a + 4)
                for j in range(RB):
                    mm = te.matmul(att_ps[0][:], v_n[:, j, :], probs_t[:, j, :],
                                   start=(j == 0), stop=(j == RB - 1))
                mm.then_inc(pv_ready, 1)

            def mlp1(g):
                pe.wait_ge(attended, 2 * g.n + 2)
                if not isinstance(g.n, int) or g.n > 0:
                    pe.wait_ge(out_done, g.n)
                te.matmul(post_ps[0][:], w1_s[:, 0, :], h2_t[g.slot][:], start=True, stop=False)
                te.matmul(post_ps[0][:], w1_s[:, 1, :], h3_t[g.slot][:], start=False, stop=True)\
                    .then_inc(mlp_ready, 1)

            def mlp2(g):
                pe.wait_ge(z_done, 2 * g.n + 1)
                te.matmul(post_ps[1][:], w2_s[:], z1_t[:], start=True, stop=True)\
                    .then_inc(mlp_ready, 1)

            def mlp3(g):
                pe.wait_ge(z_done, 2 * g.n + 2)
                for i in range(RB):
                    mm = te.matmul(post_ps[0][:, i * C:(i + 1) * C], z2_t[:, i * P:(i + 1) * P],
                                   w3_s[:], start=True, stop=True)
                mm.then_inc(mlp_ready, 1)

            def gcn_ht(g):
                turn_h("post", 2 * g.n + 1, g, post_ps[1])

            def gcn_weights(g):
                pe.wait_ge(ht_copied["post"], g.n + 1)
                for i in range(RB):
                    mm = te.matmul(post_ps[0][:, i * C:(i + 1) * C],
                                   h_t["post"][:, i * P:(i + 1) * P], gcn_ws[:],
                                   start=True, stop=True)
                mm.then_inc(gcn_ready, 1)

            def gcn_prop(g):
                pe.wait_ge(u2_done, g.n + 1)
                propagate(g, post_ps[1], u2).then_inc(gcn_ready, 1)

            def last_prop(g):
                pe.wait_ge(h_ready["post"], 2 * g.n + 2)
                propagate(g, post_ps[0], h_nat["post"]).then_inc(last_ready, 1)

            steps = {"turn_a01": lambda g: turn_a(g, (0, 1)), "turn_a23": lambda g: turn_a(g, (2, 3)),
                     "cheb_ht": cheb_ht, "cheb_weights": cheb_weights, "cheb_prop3": cheb_prop3,
                     "cheb_prop2": cheb_prop2, "cheb_prop1": cheb_prop1, "enc_ht": enc_ht,
                     "encode": encode, "queries_keys": queries_keys, "values": values,
                     "scores01": scores01, "turn0_scores2": turn0_scores2,
                     "turn1_scores3": turn1_scores3, "turn2": turn2, "turn3": turn3,
                     "attend": attend, "mlp1": mlp1, "mlp2": mlp2, "mlp3": mlp3, "gcn_ht": gcn_ht,
                     "gcn_weights": gcn_weights, "gcn_prop": gcn_prop, "last_prop": last_prop}
            rounds(pe, walk(steps))


_INS = ["x", "adj", "L0_gnn_weight", "L0_gnn_bias", "L1_gnn_enc_w", "L1_gnn_enc_b",
        "L1_gnn_a1_wv", "L1_gnn_a1_bv", "L1_gnn_a1_wk", "L1_gnn_a1_bk", "L1_gnn_a1_wq", "L1_gnn_a1_bq",
        "L1_gnn_a2_wv", "L1_gnn_a2_bv", "L1_gnn_a2_wk", "L1_gnn_a2_bk", "L1_gnn_a2_wq", "L1_gnn_a2_bq",
        "L1_gnn_m_w1", "L1_gnn_m_b1", "L1_gnn_m_w2", "L1_gnn_m_b2", "L1_gnn_m_w3", "L1_gnn_m_b3",
        "L2_gnn_kernel"]


def kernel(**inputs):
    import numpy as _np
    import concourse.bacc as _bacc
    from concourse import mybir as _mybir
    from concourse.bass_utils import run_bass_kernel_spmd as _run

    nc = _bacc.Bacc("TRN2", target_bir_lowering=False, num_devices=1)
    arrays, a = {}, {}
    for name in _INS:
        v = _np.ascontiguousarray(inputs[name])
        arrays[f"in_{name}"] = v
        a[name] = nc.dram_tensor(f"in_{name}", v.shape, _mybir.dt.from_np(v.dtype),
                                 kind="ExternalInput").ap()
    out = nc.dram_tensor("out_0", inputs["x"].shape, _mybir.dt.float32, kind="ExternalOutput").ap()
    att_w = [[a[f"L1_gnn_a{k}_w{s}"] for s in "vkq"] for k in (1, 2)]
    att_b = [[a[f"L1_gnn_a{k}_b{s}"] for s in "vkq"] for k in (1, 2)]
    graph_layers(nc, a["x"], a["adj"], a["L0_gnn_weight"], a["L0_gnn_bias"], a["L1_gnn_enc_w"],
                 a["L1_gnn_enc_b"], att_w, att_b, a["L1_gnn_m_w1"], a["L1_gnn_m_b1"],
                 a["L1_gnn_m_w2"], a["L1_gnn_m_b2"], a["L1_gnn_m_w3"], a["L1_gnn_m_b3"],
                 a["L2_gnn_kernel"], out)
    r = _run(nc, [arrays], core_ids=[0])
    return r.results[0]["out_0"]
```

```python
from contextlib import ExitStack

import numpy as np

import concourse.bass as bass
from concourse import mybir

F32 = mybir.dt.float32
F32R = mybir.dt.float32r
BF16 = mybir.dt.bfloat16
ALU = mybir.AluOpType
ACT = mybir.ActivationFunctionType

P = 128
SLOTS = 3
EPS = 1e-5
NEG = 9000000000000000.0
TINY = float(np.finfo(np.float32).tiny)

ORDER = {
    "tensor": """
        queries_keys.1 mlp1 values.1 scores0.1 turn_a0 scores1.1 scores2.1 mlp2 turn_a1 mlp3 turn0.1
        scores3.1 turn1.1 turn2.1 turn_a2 turn_a3 gcn_ht turn3.1 gcn_weights spread_inv.1 attend.1
        cheb_ht gcn_prop queries_keys.2 cheb_weights values.2 gcn_fold scores0.2 scores1.2
        cheb_prop3 cheb_fold3 scores2.2 cheb_prop2 cheb_fold2 turn0.2 scores3.2 turn1.2 cheb_prop1
        cheb_fold1 last_prop turn2.2 turn3.2 spread_inv.2 attend.2 enc_ht last_fold encode""".split(),
    "scalar": """
        queries_keys.1 values.1 mlp1 copy_at0 mlp2 row_sum0 copy_at1 row_sum1 exp0.1 exp1.1
        copy_pt0.1 exp2.1 copy_pt1.1 exp3.1 copy_pt2.1 copy_at2 gcn_ht copy_pt3.1 row_sum2 copy_at3
        row_sum3 copy_inv.1 cheb_ht gcn_copy queries_keys.2 values.2 exp0.2 cheb_copy3 cheb_copy2
        exp1.2 copy_pt0.2 exp2.2 copy_pt1.2 cheb_copy1 exp3.2 copy_pt2.2 copy_pt3.2 copy_inv.2
        last_copy enc_ht encode""".split(),
    "vector": """
        stats_cheb norm_cheb mask0.1 mask1.1 mask2.1 split_at0 split_at1 mlp3 stats_gcn split_pt0.1
        mask3.1 norm_gcn split_pt1.1 split_pt2.1 invert.1 split_pt3.1 gcn_weights split_at2 attend.1
        split_at3 cheb_ht cheb_weights mask0.2 gcn_fold mask1.2 cheb_fold3 stats_last mask2.2
        cheb_fold2 norm_last split_pt0.2 mask3.2 split_pt1.2 cheb_fold1 stats_enc split_pt2.2
        invert.2 split_pt3.2 norm_enc enc_ht attend.2 last_fold""".split(),
    "gpsimd": """
        mask_bias split_qk.1 norm_cheb add_cheb_bias norm_gcn split_v.1 inverse_roots split_qk.2
        norm_last split_v.2 norm_enc add_mlp_bias""".split(),
}


class Graph:

    def __init__(self, turn, off):
        self.n = SLOTS * turn + off
        self.slot = off % SLOTS
        self.round = turn + off // SLOTS


class Chain:

    def __init__(self, sem, per_graph):
        self.sem, self.per, self.made = sem, per_graph, 0

    def begin(self, g):
        self.base, self.made = self.per * g.n, 0

    def add(self, ins):
        ins.then_inc(self.sem, 1)
        self.made += 1
        assert self.made <= self.per

    def so_far(self):
        return self.base + self.made

    def end(self):
        assert self.made == self.per, (self.made, self.per)


def graph_layers(nc, x, adj, cheb_w, cheb_b, enc_w, enc_b, att_w, att_b, w1, b1, w2, b2, w3, b3,
                 gcn_w, out):
    B, N, C = x.shape
    H = enc_w.shape[1]
    K = cheb_w.shape[0]
    RB = N // P
    assert H == P and K == 4 and RB == 4 and 2 * C == P and B % SLOTS == 1 and B >= 7

    x_d = x.rearrange("b (i p) c -> b p i c", p=P)
    adj_d = adj.rearrange("b (i p) m -> b p i m", p=P)
    out_d = out.rearrange("b (i p) c -> b p i c", p=P)

    with ExitStack() as ctx:
        def sb(name, shape, dt=F32):
            return ctx.enter_context(nc.sbuf_tensor(name, shape, dt))

        def sem(name):
            return ctx.enter_context(nc.semaphore(name))

        ident = sb("ident", [P, P])
        ones_bf = sb("ones_bf", [P, P], BF16)
        nhalf = sb("nhalf", [P, 2 * RB])
        fold = sb("fold", [P, C])
        cheb_ws = sb("cheb_ws", [P, K, C])
        cheb_hi = sb("cheb_hi", [P, K, C], F32R)
        cheb_lo = sb("cheb_lo", [P, K, C], F32R)
        enc_ws = sb("enc_ws", [P, H])
        enc_hi = sb("enc_hi", [P, H], F32R)
        enc_lo = sb("enc_lo", [P, H], F32R)
        att_ws = [[sb(f"att_w{a}{k}", [H, H]) for k in range(3)] for a in range(2)]
        w1_s = sb("w1_s", [H, 2, H])
        w2_s = sb("w2_s", [H, H])
        w3_s = sb("w3_s", [H, C])
        gcn_ws = sb("gcn_ws", [C, C])
        enc_bs = sb("enc_bs", [H, 1])
        kq_bs = [[None] + [sb(f"kq_b{a}{k}", [H, 1]) for k in (1, 2)] for a in range(2)]
        b1_s = sb("b1_s", [H, 1])
        b2_s = sb("b2_s", [H, 1])
        cheb_bs = sb("cheb_bs", [P, C])
        b3_s = sb("b3_s", [P, C])
        bv_f = [sb(f"bv_f{a}", [P, H]) for a in range(2)]
        bv_r = [sb(f"bv_r{a}", [P, H]) for a in range(2)]
        bv_rows = [sb(f"bv_rows{a}", [P, RB, H], BF16) for a in range(2)]

        a_nat = [sb(f"a_nat{s}", [P, RB, N]) for s in range(SLOTS)]
        at_hi = [sb(f"at_hi{s}", [P, RB, N], F32R) for s in range(SLOTS)]
        at_lo = [sb(f"at_lo{s}", [P, RB, N], F32R) for s in range(SLOTS)]
        x_in = [sb(f"x_in{s}", [P, RB, C]) for s in range(SLOTS)]
        x_b = sb("x_b", [P, RB, C])
        x1 = [sb(f"x1_{s}", [P, RB, C]) for s in range(SLOTS)]
        x1b = [sb(f"x1b_{s}", [P, RB, C]) for s in range(SLOTS)]
        rs = sb("rs", [P, 2 * RB])
        dinv = [sb(f"dinv{s}", [P, 2 * RB]) for s in range(SLOTS)]
        h1_t = [sb(f"h1_t{s}", [P, N]) for s in range(SLOTS)]
        h2_t = [sb(f"h2_t{s}", [P, N]) for s in range(SLOTS)]
        h3_t = [sb(f"h3_t{s}", [P, N]) for s in range(SLOTS)]
        x_out = [sb(f"x_out{s}", [P, RB, C]) for s in range(SLOTS)]

        junk = sb("junk", [P, N], BF16)
        positive = sb("positive", [P, RB])
        d_m2 = sb("d_m2", [P, RB])
        d_neg = sb("d_neg", [P, RB])
        d_root = sb("d_root", [P, RB])
        stats = {t: sb(f"stats_{t}", [P, RB, 6]) for t in ("pre", "post")}
        meanvar = {t: sb(f"meanvar_{t}", [P, RB, 2]) for t in ("pre", "post")}
        vareps = {t: sb(f"vareps_{t}", [P, RB]) for t in ("pre", "post")}
        rstd = {t: sb(f"rstd_{t}", [P, RB]) for t in ("pre", "post")}
        centred = {t: sb(f"centred_{t}", [P, RB, C]) for t in ("pre", "post")}
        h_nat = {"pre": sb("h_nat_pre", [P, RB, 2, C]), "post": sb("h_nat_post", [P, RB, C])}
        h_t = {"pre": sb("h_t_pre", [P, N], F32R), "post": sb("h_t_post", [C, N])}
        u_pair = {t: sb(f"u_pair_{t}", [P, RB, 2, C], F32R) for t in ("pre", "post")}
        y_t = {t: sb(f"y_t_{t}", [P, N]) for t in ("pre", "post")}
        c3 = sb("c3", [P, RB, C])
        c2 = sb("c2", [P, RB, C])
        c1 = sb("c1", [P, RB, C])
        e2 = sb("e2", [P, RB, C])
        e1 = sb("e1", [P, RB, C])
        f0 = sb("f0", [P, RB, C])
        tmp = sb("tmp", [P, RB, C])
        q_t, k_t, v_n = (sb(n, [P, N]) for n in ("q_t", "k_t", "v_n"))
        q_hi, k_hi, v_hi = (sb(n, [P, N], F32R) for n in ("q_hi", "k_hi", "v_hi"))
        q_lo, k_lo, v_lo = (sb(n, [P, N], F32R) for n in ("q_lo", "k_lo", "v_lo"))
        gate = sb("gate", [P, RB, N])
        negz = sb("negz", [P, RB, N])
        negmax = sb("negmax", [P, RB])
        probs = negz
        total = sb("total", [P, RB])
        inv_total = sb("inv_total", [P, RB])
        pt_hi = sb("pt_hi", [P, RB, N], F32R)
        pt_lo = sb("pt_lo", [P, RB, N], F32R)
        inv_row = sb("inv_row", [P, N])
        z1_t = sb("z1_t", [P, N])
        z2_t = sb("z2_t", [P, N])
        x2 = sb("x2", [P, RB, C])
        x3 = sb("x3", [P, RB, C])
        u2 = sb("u2", [P, RB, C])
        s2 = sb("s2", [P, RB, C])
        last = sb("last", [P, RB, C])

        att_ps = [ctx.enter_context(nc.psum_tensor(f"att_ps{k}", [P, N], F32)) for k in range(4)]
        pre_ps = ctx.enter_context(nc.psum_tensor("pre_ps", [P, 2, N], F32))
        post_ps = [ctx.enter_context(nc.psum_tensor(f"post_ps{k}", [P, N], F32)) for k in range(2)]

        weights_in = sem("weights_in")
        consts_done = sem("consts_done")
        bias_rows = sem("bias_rows")
        weights_split = sem("weights_split")
        a_loaded = [sem(f"a_loaded{s}") for s in range(SLOTS)]
        x_loaded = [sem(f"x_loaded{s}") for s in range(SLOTS)]
        out_sent = [sem(f"out_sent{s}") for s in range(SLOTS)]
        at_ready = sem("at_ready")
        ht_ready = {t: sem(f"ht_ready_{t}") for t in ("pre", "post")}
        cheb_ready = sem("cheb_ready")
        y_ready = {t: sem(f"y_ready_{t}") for t in ("pre", "post")}
        prop_ready = sem("prop_ready")
        enc_ready = sem("enc_ready")
        qk_ready = sem("qk_ready")
        v_ready = sem("v_ready")
        scores_ready = sem("scores_ready")
        pt_ready = sem("pt_ready")
        inv_ready = sem("inv_ready")
        pv_ready = sem("pv_ready")
        mlp_ready = sem("mlp_ready")
        gcn_ready = sem("gcn_ready")
        last_ready = sem("last_ready")
        rowsums = sem("rowsums")
        at_copied = sem("at_copied")
        ht_copied = {t: sem(f"ht_copied_{t}") for t in ("pre", "post")}
        y_copied = {t: sem(f"y_copied_{t}") for t in ("pre", "post")}
        h1_done = sem("h1_done")
        qkv_done = sem("qkv_done")
        probs_done = sem("probs_done")
        pt_copied = sem("pt_copied")
        inv_copied = sem("inv_copied")
        z_done = sem("z_done")
        var_ready = {t: sem(f"var_ready_{t}") for t in ("pre", "post")}
        h_ready = {t: sem(f"h_ready_{t}") for t in ("pre", "post")}
        at_split = sem("at_split")
        ht_split = sem("ht_split")
        u_split = {t: sem(f"u_split_{t}") for t in ("pre", "post")}
        pt_split = sem("pt_split")
        cheb_taken = sem("cheb_taken")
        c_ready = sem("c_ready")
        x1_done = sem("x1_done")
        masked = sem("masked")
        biased = sem("biased")
        inv_done = sem("inv_done")
        attended = sem("attended")
        x2_done = sem("x2_done")
        u2_done = sem("u2_done")
        x3_done = sem("x3_done")
        out_done = sem("out_done")
        dve_pre = Chain(sem("dve_pre"), 2 * 6 + 9 + 3)
        dve_post = Chain(sem("dve_post"), 2 * 5 + 3 + 2)
        gate_done = sem("gate_done")
        xb_done = sem("xb_done")
        x1b_done = sem("x1b_done")
        dinv_done = sem("dinv_done")
        qkv_split = sem("qkv_split")
        rstd_done = {t: sem(f"rstd_done_{t}") for t in ("pre", "post")}
        pool_pre = Chain(sem("pool_pre"), 7)

        def over_blocks(per_row):
            return per_row.unsqueeze(2).to_broadcast([P, RB, C])

        def over_rows(per_channel):
            return per_channel.unsqueeze(1).to_broadcast([P, RB, C])

        def rows(ps):
            return ps[:, 0:RB * C].rearrange("p (i c) -> p i c", c=C)

        def cheb_part(k):
            return pre_ps[:, :, :].rearrange("p a (i k c) -> p (a i) k c", i=RB // 2, c=C)[:, :, k, :]

        def walk(engine, steps, chains=None):
            chains = chains or {}
            stage_of = {name: stage for stage, own in steps.items() for name in own}
            for own in steps.values():
                assert [n for n in ORDER[engine] if n in own] == list(own), (engine, list(own))

            def one(g_pre, g_att, g_post):
                graphs = {"pre": g_pre, "att": g_att, "post": g_post}
                for stage, chain in chains.items():
                    if graphs[stage] is not None:
                        chain.begin(graphs[stage])
                for name in ORDER[engine]:
                    g = graphs[stage_of[name]]
                    if g is not None:
                        steps[stage_of[name]][name](g)
                for stage, chain in chains.items():
                    if graphs[stage] is not None:
                        chain.end()
            return one

        def layers(**steps):
            def bind(f, a):
                return lambda g: f(g, a)
            return {f"{name}.{a + 1}": bind(f, a) for a in range(2) for name, f in steps.items()}

        def rounds(eng, one):
            one(Graph(0, 0), None, None)
            one(Graph(0, 1), Graph(0, 0), None)
            one(Graph(0, 2), Graph(0, 1), Graph(0, 0))
            with eng.Fori(0, (B - 4) // SLOTS) as turn:
                for u in range(2, 2 + SLOTS):
                    one(Graph(turn, u + 1), Graph(turn, u), Graph(turn, u - 1))
            one(Graph(0, B - 1), Graph(0, B - 2), Graph(0, B - 3))
            one(None, Graph(0, B - 1), Graph(0, B - 2))
            one(None, None, Graph(0, B - 1))

        held = sem("held")

        def hold(eng):
            eng.sem_inc(held)

        block = ctx.enter_context(nc.Block())

        @block.sync
        def _(sp):
            small = [(half, cheb_w.rearrange("k o c d -> (o c) k d"))
                     for half in (cheb_ws[0:C], cheb_ws[C:P])]
            small += [(half, enc_w) for half in (enc_ws[0:C], enc_ws[C:P])]
            small += [(w1_s[:], w1.rearrange("(a h) n -> h a n", a=2)),
                     (w2_s[:], w2), (w3_s[:], w3), (gcn_ws[:], gcn_w),
                     (enc_bs[:], enc_b.rearrange("(h o) -> h o", o=1)),
                     (b1_s[:], b1.rearrange("(h o) -> h o", o=1)),
                     (b2_s[:], b2.rearrange("(h o) -> h o", o=1)),
                     (cheb_bs[:], cheb_b.rearrange("a b c -> (a b c)").partition_broadcast(P)),
                     (b3_s[:], b3.partition_broadcast(P))]
            for a in range(2):
                small += [(att_ws[a][k][:], att_w[a][k]) for k in range(3)]
                small += [(kq_bs[a][k][:], att_b[a][k].rearrange("(h o) -> h o", o=1)) for k in (1, 2)]
                small += [(bv_f[a][:], att_b[a][0].partition_broadcast(P))]

            def load(g, waits=True):
                if waits:
                    sp.wait_ge(biased, 8 * (g.n - SLOTS) + 8)
                    hold(sp)
                    sp.wait_ge(x1_done, g.n - SLOTS + 1)
                sp.dma_start(x_in[g.slot][:], x_d[g.n]).then_inc(x_loaded[g.slot], 16)
                sp.dma_start(a_nat[g.slot][:], adj_d[g.n]).then_inc(a_loaded[g.slot], 16)

            def store(g):
                sp.wait_ge(out_done, g.n + 1)
                sp.dma_start(out_d[g.n], x_out[g.slot][:]).then_inc(out_sent[g.slot], 16)

            load(Graph(0, 0), False)
            for to, what in small:
                sp.dma_start(to, what).then_inc(weights_in, 16)
            load(Graph(0, 1), False)
            load(Graph(0, 2), False)
            load(Graph(0, 3))
            store(Graph(0, 0))
            with sp.Fori(0, (B - 4) // SLOTS) as turn:
                for u in range(2, 2 + SLOTS):
                    load(Graph(turn, u + 2))
                    store(Graph(turn, u - 1))
            for n in range(B - 3, B):
                store(Graph(0, n))
            for s in range(SLOTS):
                sp.wait_ge(out_sent[s], 16 * len(range(s, B, SLOTS)))

        n_small = 13 + 2 * 6
        n_bias_rows = 2 * (3 + 2 + 1 + 2 + 1 + RB - 1)

        @block.gpsimd
        def _(pool):
            gp = nc.gpsimd
            gp.memset(ident[:], 0.0).then_inc(consts_done, 1)
            gp.memset(ones_bf[:], 1.0).then_inc(consts_done, 1)
            gp.memset(nhalf[:], -0.5).then_inc(consts_done, 1)
            for a in range(2):
                gp.memset(bv_rows[a][:], 0.0).then_inc(consts_done, 1)
            pool.wait_ge(consts_done, 5)
            gp.affine_select(out=ident[:], in_=ident[:], compare_op=ALU.not_equal, fill=1.0, base=0,
                             pattern=[[-1, P]], channel_multiplier=1).then_inc(consts_done, 1)
            pool.wait_ge(consts_done, 6)
            gp.tensor_tensor(fold[:], ident[:, 0:C], ident[:, C:P], ALU.add).then_inc(consts_done, 1)
            pool.wait_ge(weights_in, 16 * n_small)

            def scale_norm(t, k):
                def f(g):
                    pool.wait_ge(var_ready[t], 2 * g.n + k + 1)
                    gp.tensor_tensor(rstd[t][:], vareps[t][:], nhalf[:, 0:RB], ALU.pow)\
                        .then_inc(rstd_done[t], 1)
                    src = {"pre": (x_in[g.slot], x1[g.slot]), "post": (x2, x3)}[t][k]
                    gp.tensor_tensor(centred[t][:], src[:], meanvar[t][:, :, 0:1].to_broadcast([P, RB, C]),
                                     ALU.subtract).then_inc(rstd_done[t], 1)
                return f

            def add_cheb_bias(g):
                pool.wait_ge(x_loaded[g.slot], 16 * (g.round + 1))
                if not isinstance(g.n, int) or g.n > 0:
                    pool.wait_ge(x1_done, g.n)
                gp.tensor_tensor(x_b[:], x_in[g.slot][:], over_rows(cheb_bs[:]), ALU.add)\
                    .then_inc(xb_done, 1)

            def inverse_roots(g):
                pool.wait_ge(rowsums, 4 * g.n + 4)
                hold(pool)
                d = dinv[g.slot]
                pool_pre.add(gp.tensor_scalar(rs[:, RB:], rs[:, 0:RB], 1.0, TINY, ALU.add, ALU.max))
                pool_pre.add(gp.tensor_scalar(positive[:], rs[:, 0:RB], 1.0, 0.0, ALU.add, ALU.is_gt))
                pool.wait_ge(pool_pre.sem, pool_pre.so_far())
                pool_pre.add(gp.tensor_tensor(d[:], rs[:], nhalf[:], ALU.pow))
                pool.wait_ge(pool_pre.sem, pool_pre.so_far())
                pool_pre.add(gp.tensor_tensor(d[:, RB:], d[:, RB:], positive[:], ALU.mult))
                pool_pre.add(gp.tensor_scalar(d_neg[:], d[:, 0:RB], -1.0, None, ALU.mult))
                pool_pre.add(gp.tensor_tensor(d_root[:], d[:, 0:RB], rs[:, 0:RB], ALU.mult))
                pool_pre.add(gp.tensor_scalar(d_m2[:], d[:, 0:RB], -2.0, None, ALU.mult))
                pool.wait_ge(pool_pre.sem, pool_pre.so_far())
                gp.tensor_tensor(d_m2[:], d_m2[:], d[:, 0:RB], ALU.mult).then_inc(dinv_done, 1)

            def mask_bias(g):
                if not isinstance(g.n, int) or g.n > 0:
                    pool.wait_ge(biased, 8 * g.n)
                    hold(pool)
                gp.tensor_scalar(gate[:], a_nat[g.slot][:], -1.0, NEG, ALU.add, ALU.mult)\
                    .then_inc(gate_done, 1)

            def split(whole, high, low, g, a, k):
                pool.wait_ge(qkv_done, 12 * g.n + 6 * a + 2 * k + 2)
                gp.tensor_tensor(low[:], whole[:], high[:].bitcast(F32), ALU.subtract)\
                    .then_inc(qkv_split, 1)

            def queries_keys(g, a):
                split(q_t, q_hi, q_lo, g, a, 0)
                split(k_t, k_hi, k_lo, g, a, 1)

            def values(g, a):
                split(v_n, v_hi, v_lo, g, a, 2)

            def add_mlp_bias(g):
                pool.wait_ge(x1_done, g.n + 1)
                gp.tensor_tensor(x1b[g.slot][:], x1[g.slot][:], over_rows(b3_s[:]), ALU.add)\
                    .then_inc(x1b_done, 1)

            rounds(pool, walk("gpsimd", {
                "pre": {"norm_cheb": scale_norm("pre", 0), "add_cheb_bias": add_cheb_bias,
                        "inverse_roots": inverse_roots, "norm_enc": scale_norm("pre", 1),
                        "add_mlp_bias": add_mlp_bias},
                "att": {"mask_bias": mask_bias, **layers(split_qk=queries_keys, split_v=values)},
                "post": {"norm_gcn": scale_norm("post", 0), "norm_last": scale_norm("post", 1)},
            }, {"pre": pool_pre}))

        @block.scalar
        def _(act):
            sc = nc.scalar
            act.wait_ge(weights_in, 16 * n_small)

            def copy_at(j):
                def f(g):
                    act.wait_ge(at_ready, 4 * g.n + j + 1)
                    sc.activation(at_hi[g.slot][:, j, :], pre_ps[:, j % 2, :], ACT.Copy)\
                        .then_inc(at_copied, 1)
                return f

            def row_sum(i):
                def f(g):
                    if i == 0:
                        act.wait_ge(a_loaded[g.slot], 16 * (g.round + 1))
                        if not isinstance(g.n, int) or g.n > 0:
                            act.wait_ge(dinv_done, g.n)
                    if i or not isinstance(g.n, int) or g.n > 0:
                        act.wait_ge(rowsums, 4 * g.n + i)
                    sc.activation(junk[:], a_nat[g.slot][:, i, :], ACT.Copy,
                                  accum_out=rs[:, i:i + 1]).then_inc(rowsums, 1)
                return f

            def copy_ht(t, k, per, ps):
                def f(g):
                    act.wait_ge(ht_ready[t], per * g.n + k + 1)
                    sc.activation(h_t[t][:], ps, ACT.Copy).then_inc(ht_copied[t], 1)
                return f

            def copy_y(t, k, per, ps):
                def f(g):
                    act.wait_ge(y_ready[t], per * g.n + k + 1)
                    sc.activation(y_t[t][:], ps, ACT.Copy).then_inc(y_copied[t], 1)
                return f

            def encode(g):
                act.wait_ge(enc_ready, g.n + 1)
                sc.activation(h1_t[g.slot][:], pre_ps[:, 1, :], ACT.Tanh, bias=enc_bs[:])\
                    .then_inc(h1_done, 1)

            def queries_keys(g, a):
                for k, (whole, high, which) in enumerate(((q_t, q_hi, 2), (k_t, k_hi, 1))):
                    act.wait_ge(qk_ready, 4 * g.n + 2 * a + k + 1)
                    for to in (high, whole):
                        sc.activation(to[:], att_ps[k][:], ACT.Tanh, bias=kq_bs[a][which][:])\
                            .then_inc(qkv_done, 1)

            def values(g, a):
                act.wait_ge(v_ready, 2 * g.n + a + 1)
                for to in (v_hi, v_n):
                    sc.activation(to[:], att_ps[2][:], ACT.Tanh).then_inc(qkv_done, 1)

            def exponent(i):
                def f(g, a):
                    act.wait_ge(biased, 8 * g.n + 4 * a + i + 1)
                    sc.activation(probs[:, i, :], negz[:, i, :], ACT.Exp, bias=negmax[:, i:i + 1],
                                  scale=-1.0, accum_out=total[:, i:i + 1]).then_inc(probs_done, 1)
                return f

            def copy_pt(i):
                def f(g, a):
                    act.wait_ge(pt_ready, 8 * g.n + 4 * a + i + 1)
                    sc.activation(pt_hi[:, :, i * P:(i + 1) * P],
                                  att_ps[2 + i % 2][:].rearrange("p (j n) -> p j n", n=P), ACT.Copy)\
                        .then_inc(pt_copied, 1)
                return f

            def copy_inv(g, a):
                act.wait_ge(inv_ready, 2 * g.n + a + 1)
                sc.activation(inv_row[:], att_ps[1][:], ACT.Copy).then_inc(inv_copied, 1)

            def mlp(k, to, ps, bias):
                def f(g):
                    act.wait_ge(mlp_ready, 3 * g.n + k + 1)
                    sc.activation(to[:], ps[:], ACT.Relu, bias=bias[:]).then_inc(z_done, 1)
                return f

            rounds(act, walk("scalar", {
                "pre": {"copy_at0": copy_at(0), "row_sum0": row_sum(0), "copy_at1": copy_at(1),
                        "row_sum1": row_sum(1), "copy_at2": copy_at(2), "row_sum2": row_sum(2),
                        "copy_at3": copy_at(3), "row_sum3": row_sum(3),
                        "cheb_ht": copy_ht("pre", 0, 2, pre_ps[:, 0, :]),
                        "cheb_copy3": copy_y("pre", 0, 3, pre_ps[:, 0, :]),
                        "cheb_copy2": copy_y("pre", 1, 3, pre_ps[:, 0, :]),
                        "cheb_copy1": copy_y("pre", 2, 3, pre_ps[:, 0, :]),
                        "enc_ht": copy_ht("pre", 1, 2, pre_ps[:, 0, :]),
                        "encode": encode},
                "att": layers(queries_keys=queries_keys, values=values, exp0=exponent(0),
                              exp1=exponent(1), copy_pt0=copy_pt(0), exp2=exponent(2),
                              copy_pt1=copy_pt(1), exp3=exponent(3), copy_pt2=copy_pt(2),
                              copy_pt3=copy_pt(3), copy_inv=copy_inv),
                "post": {"mlp1": mlp(0, z1_t, post_ps[0], b1_s), "mlp2": mlp(1, z2_t, post_ps[1], b2_s),
                         "gcn_ht": copy_ht("post", 0, 1, post_ps[1][0:C, :]),
                         "gcn_copy": copy_y("post", 0, 2, post_ps[1][:]),
                         "last_copy": copy_y("post", 1, 2, post_ps[1][:])},
            }))

        @block.vector
        def _(dve):
            ve = nc.vector

            dve.wait_ge(weights_in, 16 * n_small)
            dve.wait_ge(consts_done, 6)
            made = 0
            for a in range(2):
                rest = bv_f[a]
                for row, p0 in enumerate((0, 32, 64)):
                    for p1 in range(p0, 96, 32):
                        ve.tensor_copy(bv_rows[a][p1:p1 + 1, 0, :], rest[p1:p1 + 1, :])\
                            .then_inc(bias_rows, 1)
                        made += 1
                    dve.wait_ge(bias_rows, made)
                    for p1 in range(p0 + 32, 96, 32):
                        ve.tensor_tensor(rest[p1:p1 + 1, :], rest[p1:p1 + 1, :],
                                         bv_rows[a][p1:p1 + 1, 0, :], ALU.subtract)\
                            .then_inc(bias_rows, 1)
                        made += 1
                    dve.wait_ge(bias_rows, made)
                for i in range(1, RB):
                    ve.tensor_copy(bv_rows[a][0:96, i, :], bv_rows[a][0:96, 0, :])\
                        .then_inc(bias_rows, 1)
                    made += 1
            assert made == n_bias_rows
            for whole, high, low in ((cheb_ws, cheb_hi, cheb_lo), (enc_ws, enc_hi, enc_lo)):
                ve.tensor_copy(high[:], whole[:]).then_inc(weights_split, 1)
            dve.wait_ge(weights_split, 2)
            for whole, high, low in ((cheb_ws, cheb_hi, cheb_lo), (enc_ws, enc_hi, enc_lo)):
                ve.tensor_tensor(low[:], whole[:], high[:].bitcast(F32), ALU.subtract)\
                    .then_inc(weights_split, 1)

            def norm_stats(t, chain, g, k, src):
                st, mv = stats[t], meanvar[t]
                for i in range(RB):
                    chain.add(ve.bn_stats(st[:, i, :], src[:, i, :]))
                dve.wait_ge(chain.sem, chain.so_far())
                hold(dve)
                for i in range(RB):
                    last_one = ve.bn_aggr(mv[:, i, :], st[:, i, :])
                chain.add(last_one)
                dve.wait_ge(chain.sem, chain.so_far())
                ve.tensor_scalar(vareps[t][:], mv[:, :, 1], EPS, None, ALU.add)\
                    .then_inc(var_ready[t], 1)

            def norm_apply(t, chain, g, k):
                dve.wait_ge(rstd_done[t], 4 * g.n + 2 * k + 2)
                to = h_nat[t][:, :, 0, :] if t == "pre" else h_nat[t][:]
                one = ve.scalar_tensor_tensor(to, centred[t][:], 0.0, over_blocks(rstd[t][:]),
                                              ALU.max, ALU.mult)
                if t == "post":
                    one.then_inc(h_ready[t], 1)
                    return
                chain.add(one)
                dve.wait_ge(chain.sem, chain.so_far())
                ve.tensor_copy(h_nat[t][:, :, 1, :], to).then_inc(h_ready[t], 1)

            def split_at(j):
                def f(g):
                    dve.wait_ge(at_copied, 4 * g.n + j + 1)
                    ve.tensor_tensor(at_lo[g.slot][:, j, :], pre_ps[:, j % 2, :],
                                     at_hi[g.slot][:, j, :].bitcast(F32), ALU.subtract)\
                        .then_inc(at_split, 1)
                return f

            def split_ht(g, k):
                dve.wait_ge(ht_copied["pre"], 2 * g.n + k + 1)
                ve.tensor_tensor(h_t["pre"][C:P, :], pre_ps[C:P, 0, :],
                                 h_t["pre"][C:P, :].bitcast(F32), ALU.subtract).then_inc(ht_split, 1)

            def split_u(t, chain, u):
                chain.add(ve.tensor_copy(u_pair[t][:, :, 0, :], u[:]))
                dve.wait_ge(chain.sem, chain.so_far())
                ve.tensor_tensor(u_pair[t][:, :, 1, :], u[:], u_pair[t][:, :, 0, :].bitcast(F32),
                                 ALU.subtract).then_inc(u_split[t], 1)

            def stats_cheb(g):
                dve.wait_ge(x_loaded[g.slot], 16 * (g.round + 1))
                norm_stats("pre", dve_pre, g, 0, x_in[g.slot])

            def cheb_norm(g):
                if not isinstance(g.n, int) or g.n > 0:
                    dve.wait_ge(ht_ready["pre"], 2 * g.n)
                norm_apply("pre", dve_pre, g, 0)

            def cheb_weights(g):
                d = over_blocks(dinv[g.slot][:, 0:RB])
                dve.wait_ge(cheb_ready, g.n + 1)
                dve.wait_ge(dinv_done, g.n + 1)
                ve.tensor_tensor(c3[:], cheb_part(3), d, ALU.mult).then_inc(cheb_taken, 1)
                ve.tensor_tensor(e2[:], cheb_part(2), d, ALU.mult).then_inc(cheb_taken, 1)
                ve.tensor_tensor(e1[:], cheb_part(1), d, ALU.mult).then_inc(cheb_taken, 1)
                dve.wait_ge(xb_done, g.n + 1)
                ve.tensor_tensor(f0[:], cheb_part(0), x_b[:], ALU.add).then_inc(cheb_taken, 1)
                dve.wait_ge(cheb_taken, 4 * g.n + 3)
                split_u("pre", dve_pre, c3)
                dve_pre.add(ve.scalar_tensor_tensor(e2[:], c3[:], 2.0, e2[:], ALU.mult, ALU.add))
                dve_pre.add(ve.tensor_tensor(e1[:], e1[:], c3[:], ALU.subtract))

            def cheb_fold3(g):
                dve.wait_ge(prop_ready, 3 * g.n + 1)
                dve_pre.add(ve.tensor_tensor(tmp[:], rows(pre_ps[:, 1, :]), over_blocks(d_m2[:]), ALU.mult))
                dve.wait_ge(dve_pre.sem, dve_pre.so_far())
                ve.tensor_tensor(c2[:], tmp[:], e2[:], ALU.add).then_inc(c_ready, 1)
                dve.wait_ge(c_ready, 2 * g.n + 1)
                split_u("pre", dve_pre, c2)
                dve_pre.add(ve.scalar_tensor_tensor(e1[:], c2[:], 2.0, e1[:], ALU.mult, ALU.add))

            def cheb_fold2(g):
                dve.wait_ge(prop_ready, 3 * g.n + 2)
                dve_pre.add(ve.tensor_tensor(tmp[:], rows(pre_ps[:, 1, :]), over_blocks(d_m2[:]), ALU.mult))
                dve.wait_ge(dve_pre.sem, dve_pre.so_far())
                ve.tensor_tensor(c1[:], tmp[:], e1[:], ALU.add).then_inc(c_ready, 1)
                dve.wait_ge(c_ready, 2 * g.n + 2)
                split_u("pre", dve_pre, c1)
                dve_pre.add(ve.tensor_tensor(tmp[:], c1[:], c2[:], ALU.subtract))
                dve.wait_ge(dve_pre.sem, dve_pre.so_far())
                dve_pre.add(ve.tensor_tensor(tmp[:], tmp[:], over_blocks(d_root[:]), ALU.mult))
                dve.wait_ge(dve_pre.sem, dve_pre.so_far())
                dve.wait_ge(cheb_taken, 4 * g.n + 4)
                dve_pre.add(ve.tensor_tensor(f0[:], f0[:], tmp[:], ALU.add))

            def cheb_fold1(g):
                dve.wait_ge(prop_ready, 3 * g.n + 3)
                dve.wait_ge(dve_pre.sem, dve_pre.so_far())
                dve_pre.add(ve.tensor_tensor(tmp[:], rows(pre_ps[:, 1, :]), over_blocks(d_neg[:]), ALU.mult))
                dve.wait_ge(dve_pre.sem, dve_pre.so_far())
                ve.tensor_tensor(x1[g.slot][:], tmp[:], f0[:], ALU.add).then_inc(x1_done, 1)

            def stats_enc(g):
                dve.wait_ge(x1_done, g.n + 1)
                norm_stats("pre", dve_pre, g, 1, x1[g.slot])

            def enc_norm(g):
                norm_apply("pre", dve_pre, g, 1)

            def mask(i):
                return lambda g, a: mask_rows(g, a, i)

            def mask_rows(g, a, i):
                n = 4 * a + i
                s = g.slot
                dve.wait_ge(scores_ready, 8 * g.n + n + 1)
                ve.tensor_tensor(negz[:, i, :], att_ps[i % 2][:], a_nat[s][:, i, :], ALU.mult)\
                    .then_inc(masked, 1)
                if n == 0:
                    dve.wait_ge(gate_done, g.n + 1)
                dve.wait_ge(masked, 8 * g.n + n + 1)
                hold(dve)
                ve.tensor_tensor_reduce(negz[:, i, :], negz[:, i, :], gate[:, i, :], -1.0, 3.0e38,
                                        ALU.add, ALU.min, negmax[:, i:i + 1]).then_inc(biased, 1)

            def split_pt(i):
                return lambda g, a: split_rows(g, a, i)

            def split_rows(g, a, i):
                dve.wait_ge(pt_copied, 8 * g.n + 4 * a + i + 1)
                part = slice(i * P, (i + 1) * P)
                ve.tensor_tensor(pt_lo[:, :, part], att_ps[2 + i % 2][:].rearrange("p (j n) -> p j n", n=P),
                                 pt_hi[:, :, part].bitcast(F32), ALU.subtract).then_inc(pt_split, 1)

            def invert(g, a):
                dve.wait_ge(probs_done, 8 * g.n + 4 * a + 4)
                ve.reciprocal(inv_total[:], total[:]).then_inc(inv_done, 1)

            def attend(g, a):
                to = (h2_t, h3_t)[a][g.slot]
                dve.wait_ge(inv_copied, 2 * g.n + a + 1)
                dve.wait_ge(pv_ready, 2 * g.n + a + 1)
                ve.tensor_tensor(to[:], att_ps[0][:], inv_row[:], ALU.mult).then_inc(attended, 1)

            def mlp3(g):
                dve.wait_ge(mlp_ready, 3 * g.n + 3)
                dve.wait_ge(x1b_done, g.n + 1)
                ve.tensor_tensor(x2[:], rows(post_ps[0][:]), x1b[g.slot][:], ALU.add).then_inc(x2_done, 1)

            def stats_gcn(g):
                dve.wait_ge(x2_done, g.n + 1)
                norm_stats("post", dve_post, g, 0, x2)

            def gcn_norm(g):
                norm_apply("post", dve_post, g, 0)

            def gcn_weights(g):
                dve.wait_ge(gcn_ready, 2 * g.n + 1)
                ve.tensor_tensor(u2[:], rows(post_ps[0][:]), over_blocks(dinv[g.slot][:, RB:]), ALU.mult)\
                    .then_inc(u2_done, 1)
                dve.wait_ge(u2_done, g.n + 1)
                split_u("post", dve_post, u2)

            def gcn_fold(g):
                dve.wait_ge(gcn_ready, 2 * g.n + 2)
                dve.wait_ge(u2_done, g.n + 1)
                dve_post.add(ve.tensor_tensor(s2[:], rows(post_ps[0][:]), u2[:], ALU.add))
                dve.wait_ge(dve_post.sem, dve_post.so_far())
                dve_post.add(ve.tensor_tensor(s2[:], s2[:], over_blocks(dinv[g.slot][:, RB:]), ALU.mult))
                dve.wait_ge(dve_post.sem, dve_post.so_far())
                ve.scalar_tensor_tensor(x3[:], s2[:], 0.0, x2[:], ALU.max, ALU.add).then_inc(x3_done, 1)

            def stats_last(g):
                dve.wait_ge(x3_done, g.n + 1)
                norm_stats("post", dve_post, g, 1, x3)

            def last_norm(g):
                norm_apply("post", dve_post, g, 1)
                dve.wait_ge(h_ready["post"], 2 * g.n + 2)
                split_u("post", dve_post, h_nat["post"])

            def last_fold(g):
                dve.wait_ge(last_ready, g.n + 1)
                dve_post.add(ve.scalar_tensor_tensor(last[:], rows(post_ps[0][:]), 0.5, x3[:],
                                                     ALU.is_gt, ALU.add))
                dve.wait_ge(dve_post.sem, dve_post.so_far())
                if not isinstance(g.n, int) or g.n >= SLOTS:
                    dve.wait_ge(out_sent[g.slot], 16 * g.round)
                ve.scalar_tensor_tensor(x_out[g.slot][:], rows(post_ps[0][:]), 0.0, last[:],
                                        ALU.mult, ALU.add).then_inc(out_done, 1)

            rounds(dve, walk("vector", {
                "pre": {"stats_cheb": stats_cheb, "norm_cheb": cheb_norm, "split_at0": split_at(0),
                        "split_at1": split_at(1), "split_at2": split_at(2), "split_at3": split_at(3),
                        "cheb_ht": lambda g: split_ht(g, 0), "cheb_weights": cheb_weights,
                        "cheb_fold3": cheb_fold3, "cheb_fold2": cheb_fold2, "cheb_fold1": cheb_fold1,
                        "stats_enc": stats_enc, "norm_enc": enc_norm,
                        "enc_ht": lambda g: split_ht(g, 1)},
                "att": layers(mask0=mask(0), mask1=mask(1), mask2=mask(2), split_pt0=split_pt(0),
                              mask3=mask(3), split_pt1=split_pt(1), split_pt2=split_pt(2),
                              invert=invert, split_pt3=split_pt(3), attend=attend),
                "post": {"mlp3": mlp3, "stats_gcn": stats_gcn, "norm_gcn": gcn_norm,
                         "gcn_weights": gcn_weights, "gcn_fold": gcn_fold,
                         "stats_last": stats_last, "norm_last": last_norm, "last_fold": last_fold},
            }, {"pre": dve_pre, "post": dve_post}))

        @block.tensor
        def _(pe):
            te = nc.tensor
            pe.wait_ge(consts_done, 7)
            pe.wait_ge(weights_split, 4)
            pe.wait_ge(weights_in, 16 * n_small)
            pe.wait_ge(bias_rows, n_bias_rows)

            def turn_a(j):
                def f(g):
                    pe.wait_ge(a_loaded[g.slot], 16 * (g.round + 1))
                    if j == 0 and (not isinstance(g.n, int) or g.n > 0):
                        pe.wait_ge(h1_done, g.n)
                    if j >= 2:
                        pe.wait_ge(at_split, 4 * g.n + j - 1)
                    for i in range(RB):
                        mm = te.transpose(pre_ps[:, j % 2, i * P:(i + 1) * P],
                                          a_nat[g.slot][:, i, j * P:(j + 1) * P], ident[:])
                    mm.then_inc(at_ready, 1)
                return f

            def turn_h(t, ready, bank):
                times = 2 if t == "pre" else 1
                pe.wait_ge(h_ready[t], ready)
                hold(pe)
                for i in range(RB):
                    src = h_nat[t][:, i, :, :].rearrange("p a c -> p (a c)") \
                        if times == 2 else h_nat[t][:, i, :]
                    mm = te.transpose(bank[0:times * C, i * P:(i + 1) * P], src, ident[:])
                mm.then_inc(ht_ready[t], 1)

            def cheb_ht(g):
                pe.wait_ge(at_split, 4 * g.n + 3)
                turn_h("pre", 2 * g.n + 1, pre_ps[:, 0, :])

            def cheb_weights(g):
                pe.wait_ge(at_split, 4 * g.n + 4)
                pe.wait_ge(ht_split, 2 * g.n + 1)
                for i in range(RB):
                    w = K * C
                    for part in (cheb_hi, cheb_lo):
                        mm = te.matmul(pre_ps[:, i // 2, i % 2 * w:(i % 2 + 1) * w],
                                       h_t["pre"][:, i * P:(i + 1) * P],
                                       part[:].rearrange("c k d -> c (k d)"),
                                       start=(part is cheb_hi), stop=(part is cheb_lo))
                mm.then_inc(cheb_ready, 1)

            def propagate(t, g, ready, bank):
                pe.wait_ge(u_split[t], ready)
                for j in range(RB):
                    for at in (at_hi, at_lo):
                        mm = te.matmul(bank, u_pair[t][:, j, :, :].rearrange("p a c -> p (a c)"),
                                       at[g.slot][:, j, :],
                                       start=(j == 0 and at is at_hi), stop=(j == RB - 1 and at is at_lo))
                mm.then_inc(y_ready[t], 1)

            def fold_up(t, ready, bank):
                pe.wait_ge(y_copied[t], ready)
                for i in range(RB):
                    mm = te.matmul(bank[:, i * C:(i + 1) * C], y_t[t][:, i * P:(i + 1) * P], fold[:],
                                   start=True, stop=True)
                return mm

            def cheb_prop3(g):
                pe.wait_ge(cheb_taken, 4 * g.n + 4)
                propagate("pre", g, 3 * g.n + 1, pre_ps[:, 0, :])

            def cheb_prop(k):
                return lambda g: propagate("pre", g, 3 * g.n + k, pre_ps[:, 0, :])

            def cheb_fold(k):
                return lambda g: fold_up("pre", 3 * g.n + k, pre_ps[:, 1, :]).then_inc(prop_ready, 1)

            def enc_ht(g):
                turn_h("pre", 2 * g.n + 2, pre_ps[:, 0, :])

            def encode(g):
                pe.wait_ge(ht_split, 2 * g.n + 2)
                te.matmul(pre_ps[:, 1, :], enc_hi[:], h_t["pre"][:], start=True, stop=False)
                te.matmul(pre_ps[:, 1, :], enc_lo[:], h_t["pre"][:], start=False, stop=True)\
                    .then_inc(enc_ready, 1)

            def source(g, a):
                return (h1_t, h2_t)[a][g.slot]

            def queries_keys(g, a):
                if a == 0:
                    pe.wait_ge(h1_done, g.n + 1)
                    if not isinstance(g.n, int) or g.n > 0:
                        pe.wait_ge(attended, 2 * g.n)
                else:
                    pe.wait_ge(attended, 2 * g.n + 1)
                for k, which in enumerate((2, 1)):
                    te.matmul(att_ps[k][:], att_ws[a][which][:], source(g, a)[:],
                              start=True, stop=True).then_inc(qk_ready, 1)

            def values(g, a):
                te.matmul(att_ps[2][:], ones_bf[:, :],
                          bv_rows[a][:].rearrange("p i h -> p (i h)"), start=True, stop=False,
                          skip_group_check=True)
                for i in range(RB):
                    mm = te.matmul(att_ps[2][:, i * P:(i + 1) * P],
                                   source(g, a)[:, i * P:(i + 1) * P], att_ws[a][0][:],
                                   start=False, stop=(i == RB - 1), skip_group_check=True)
                mm.then_inc(v_ready, 1)

            def scores(i):
                return lambda g, a: scores_rows(g, a, i)

            def scores_rows(g, a, i):
                if i < 2:
                    pe.wait_ge(qkv_split, 6 * g.n + 3 * a + 2)
                else:
                    pe.wait_ge(masked, 8 * g.n + 4 * a + i - 1)
                part = slice(i * P, (i + 1) * P)
                te.matmul(att_ps[i % 2][:], q_hi[:, part], k_hi[:], start=True, stop=False)
                te.matmul(att_ps[i % 2][:], q_hi[:, part], k_lo[:], start=False, stop=False)
                te.matmul(att_ps[i % 2][:], q_lo[:, part], k_hi[:], start=False, stop=True)\
                    .then_inc(scores_ready, 1)

            def turn_probs(i):
                return lambda g, a: turn_rows(g, a, i)

            def turn_rows(g, a, i):
                pe.wait_ge(probs_done, 8 * g.n + 4 * a + i + 1)
                if i == 0:
                    pe.wait_ge(qkv_done, 12 * g.n + 6 * a + 6)
                if i >= 2:
                    pe.wait_ge(pt_split, 8 * g.n + 4 * a + i - 1)
                for j in range(RB):
                    mm = te.transpose(att_ps[2 + i % 2][:, j * P:(j + 1) * P],
                                      probs[:, i, j * P:(j + 1) * P], ident[:])
                mm.then_inc(pt_ready, 1)

            def spread_inv(g, a):
                pe.wait_ge(inv_done, 2 * g.n + a + 1)
                for i in range(RB):
                    mm = te.transpose(att_ps[1][:, i * P:(i + 1) * P],
                                      inv_total[:, i:i + 1].to_broadcast([P, P]), ident[:])
                mm.then_inc(inv_ready, 1)

            def attend(g, a):
                pe.wait_ge(qkv_split, 6 * g.n + 3 * a + 3)
                pe.wait_ge(pt_split, 8 * g.n + 4 * a + 4)
                for j in range(RB):
                    part = slice(j * P, (j + 1) * P)
                    te.matmul(att_ps[0][:], v_hi[:, part], pt_hi[:, j, :], start=(j == 0), stop=False)
                    te.matmul(att_ps[0][:], v_hi[:, part], pt_lo[:, j, :], start=False, stop=False)
                    mm = te.matmul(att_ps[0][:], v_lo[:, part], pt_hi[:, j, :],
                                   start=False, stop=(j == RB - 1))
                mm.then_inc(pv_ready, 1)

            def mlp1(g):
                pe.wait_ge(attended, 2 * g.n + 2)
                if not isinstance(g.n, int) or g.n > 0:
                    pe.wait_ge(out_done, g.n)
                te.matmul(post_ps[0][:], w1_s[:, 0, :], h2_t[g.slot][:], start=True, stop=False)
                te.matmul(post_ps[0][:], w1_s[:, 1, :], h3_t[g.slot][:], start=False, stop=True)\
                    .then_inc(mlp_ready, 1)

            def mlp2(g):
                pe.wait_ge(z_done, 2 * g.n + 1)
                te.matmul(post_ps[1][:], w2_s[:], z1_t[:], start=True, stop=True)\
                    .then_inc(mlp_ready, 1)

            def mlp3(g):
                pe.wait_ge(z_done, 2 * g.n + 2)
                for i in range(RB):
                    mm = te.matmul(post_ps[0][:, i * C:(i + 1) * C], z2_t[:, i * P:(i + 1) * P],
                                   w3_s[:], start=True, stop=True)
                mm.then_inc(mlp_ready, 1)

            def gcn_ht(g):
                turn_h("post", 2 * g.n + 1, post_ps[1])

            def gcn_weights(g):
                pe.wait_ge(ht_copied["post"], g.n + 1)
                for i in range(RB):
                    mm = te.matmul(post_ps[0][:, i * C:(i + 1) * C],
                                   h_t["post"][:, i * P:(i + 1) * P], gcn_ws[:],
                                   start=True, stop=True)
                mm.then_inc(gcn_ready, 1)

            def gcn_prop(g):
                propagate("post", g, 2 * g.n + 1, post_ps[1][:])

            def gcn_fold(g):
                fold_up("post", 2 * g.n + 1, post_ps[0]).then_inc(gcn_ready, 1)

            def last_prop(g):
                propagate("post", g, 2 * g.n + 2, post_ps[1][:])

            def last_fold(g):
                fold_up("post", 2 * g.n + 2, post_ps[0]).then_inc(last_ready, 1)

            rounds(pe, walk("tensor", {
                "pre": {"turn_a0": turn_a(0), "turn_a1": turn_a(1), "turn_a2": turn_a(2),
                        "turn_a3": turn_a(3), "cheb_ht": cheb_ht, "cheb_weights": cheb_weights,
                        "cheb_prop3": cheb_prop3, "cheb_fold3": cheb_fold(1),
                        "cheb_prop2": cheb_prop(2), "cheb_fold2": cheb_fold(2),
                        "cheb_prop1": cheb_prop(3), "cheb_fold1": cheb_fold(3),
                        "enc_ht": enc_ht, "encode": encode},
                "att": layers(queries_keys=queries_keys, values=values, scores0=scores(0),
                              scores1=scores(1), scores2=scores(2), turn0=turn_probs(0),
                              scores3=scores(3), turn1=turn_probs(1), turn2=turn_probs(2),
                              turn3=turn_probs(3), spread_inv=spread_inv, attend=attend),
                "post": {"mlp1": mlp1, "mlp2": mlp2, "mlp3": mlp3, "gcn_ht": gcn_ht,
                         "gcn_weights": gcn_weights, "gcn_prop": gcn_prop, "gcn_fold": gcn_fold,
                         "last_prop": last_prop, "last_fold": last_fold},
            }))


_INS = ["x", "adj", "L0_gnn_weight", "L0_gnn_bias", "L1_gnn_enc_w", "L1_gnn_enc_b",
        "L1_gnn_a1_wv", "L1_gnn_a1_bv", "L1_gnn_a1_wk", "L1_gnn_a1_bk", "L1_gnn_a1_wq", "L1_gnn_a1_bq",
        "L1_gnn_a2_wv", "L1_gnn_a2_bv", "L1_gnn_a2_wk", "L1_gnn_a2_bk", "L1_gnn_a2_wq", "L1_gnn_a2_bq",
        "L1_gnn_m_w1", "L1_gnn_m_b1", "L1_gnn_m_w2", "L1_gnn_m_b2", "L1_gnn_m_w3", "L1_gnn_m_b3",
        "L2_gnn_kernel"]


def kernel(**inputs):
    import numpy as _np
    import concourse.bacc as _bacc
    from concourse import mybir as _mybir
    from concourse.bass_utils import run_bass_kernel_spmd as _run

    nc = _bacc.Bacc("TRN2", target_bir_lowering=False, num_devices=1)
    arrays, a = {}, {}
    for name in _INS:
        v = _np.ascontiguousarray(inputs[name])
        arrays[f"in_{name}"] = v
        a[name] = nc.dram_tensor(f"in_{name}", v.shape, _mybir.dt.from_np(v.dtype),
                                 kind="ExternalInput").ap()
    out = nc.dram_tensor("out_0", inputs["x"].shape, _mybir.dt.float32, kind="ExternalOutput").ap()
    att_w = [[a[f"L1_gnn_a{k}_w{s}"] for s in "vkq"] for k in (1, 2)]
    att_b = [[a[f"L1_gnn_a{k}_b{s}"] for s in "vkq"] for k in (1, 2)]
    graph_layers(nc, a["x"], a["adj"], a["L0_gnn_weight"], a["L0_gnn_bias"], a["L1_gnn_enc_w"],
                 a["L1_gnn_enc_b"], att_w, att_b, a["L1_gnn_m_w1"], a["L1_gnn_m_b1"],
                 a["L1_gnn_m_w2"], a["L1_gnn_m_b2"], a["L1_gnn_m_w3"], a["L1_gnn_m_b3"],
                 a["L2_gnn_kernel"], out)
    r = _run(nc, [arrays], core_ids=[0])
    return r.results[0]["out_0"]
```

```python
from contextlib import ExitStack

import numpy as np

import concourse.bass as bass
from concourse import mybir

F32 = mybir.dt.float32
F32R = mybir.dt.float32r
BF16 = mybir.dt.bfloat16
ALU = mybir.AluOpType
ACT = mybir.ActivationFunctionType

P = 128
SLOTS = 3
EPS = 1e-5
NEG = 9000000000000000.0
TINY = float(np.finfo(np.float32).tiny)

ORDER = {
    "tensor": """
        queries.1-1 turn_a0-0 turn2.2-2 turn3.2-2 keys.1-1 turn_a1-0 spread_inv.2-2 values.1-1
        turn_a2-0 turn_a3-0 attend.2-2 scores0.1-1 cheb_ht-0 scores1.1-1 scores2.1-1 mlp1-2
        turn0.1-1 cheb_weights-0 scores3.1-1 turn1.1-1 mlp2-2 turn2.1-1 cheb_prop3-0 turn3.1-1
        mlp3-2 cheb_fold3-0 spread_inv.1-1 attend.1-1 cheb_prop2-0 queries.2-1 cheb_fold2-0
        gcn_prop-2 keys.2-1 gcn_fold-2 cheb_prop1-0 scores0.2-1 cheb_fold1-0 values.2-1 scores1.2-1
        scores2.2-1 turn0.2-1 last_prop-2 enc_ht-0 scores3.2-1 turn1.2-1 encode-0 last_fold-2""".split(),
    "scalar": """
        exp3.2-2 queries.1-1 copy_pt2.2-2 copy_pt3.2-2 copy_at0-0 keys.1-1 row_sum0-0 copy_at1-0
        row_sum1-0 values.1-1 copy_at2-0 row_sum2-0 copy_at3-0 copy_inv.2-2 row_sum3-0 cheb_ht-0
        exp0.1-1 exp1.1-1 copy_pt0.1-1 mlp1-2 exp2.1-1 copy_pt1.1-1 mlp2-2 exp3.1-1 copy_pt2.1-1
        cheb_copy3-0 copy_pt3.1-1 copy_inv.1-1 cheb_copy2-0 queries.2-1 gcn_copy-2 keys.2-1
        cheb_copy1-0 values.2-1 exp0.2-1 exp1.2-1 copy_pt0.2-1 enc_ht-0 last_copy-2 exp2.2-1
        encode-0 copy_pt1.2-1""".split(),
    "vector": """
        stats_cheb-0 split_pt2.2-2 invert.2-2 split_pt3.2-2 norm_cheb-0 split_at0-0 split_at1-0
        split_at2-0 split_at3-0 attend.2-2 mask0.1-1 mask1.1-1 cheb_ht-0 mask2.1-1 split_pt0.1-1
        cheb_weights-0 mask3.1-1 split_pt1.1-1 split_pt2.1-1 invert.1-1 split_pt3.1-1 mlp3-2
        cheb_fold3-0 stats_gcn-2 attend.1-1 norm_gcn-2 cheb_fold2-0 gcn_fold-2 stats_last-2
        mask0.2-1 cheb_fold1-0 stats_enc-0 norm_last-2 mask1.2-1 norm_enc-0 mask2.2-1 enc_ht-0
        split_pt0.2-1 mask3.2-1 split_pt1.2-1 last_fold-2""".split(),
    "gpsimd": """
        norm_cheb-0 add_cheb_bias-0 split_qk.1-1 split_v.1-1 mask_bias.1-1 inverse_roots-0 cheb_u3-0
        norm_gcn-2 mask_bias.2-1 split_qk.2-1 cheb_f0-0 norm_last-2 norm_enc-0 split_v.2-1
        add_mlp_bias-0""".split(),
}


class Graph:

    def __init__(self, turn, off):
        self.n = SLOTS * turn + off
        self.slot = off % SLOTS
        self.round = turn + off // SLOTS


class Chain:

    def __init__(self, sem, per_graph):
        self.sem, self.per, self.made = sem, per_graph, [0] * SLOTS

    def next_round(self):
        assert self.made[-1] in (0, self.per), (self.made, self.per)
        self.made = [0] + self.made[:-1]

    def turn_to(self, g, age):
        self.base, self.age = self.per * g.n, age

    def add(self, ins):
        ins.then_inc(self.sem, 1)
        self.made[self.age] += 1
        assert self.made[self.age] <= self.per

    def so_far(self):
        return self.base + self.made[self.age]


def graph_layers(nc, x, adj, cheb_w, cheb_b, enc_w, enc_b, att_w, att_b, w1, b1, w2, b2, w3, b3,
                 gcn_w, out):
    B, N, C = x.shape
    H = enc_w.shape[1]
    K = cheb_w.shape[0]
    RB = N // P
    assert H == P and K == 4 and RB == 4 and 2 * C == P and B % SLOTS == 1 and B >= 7

    x_d = x.rearrange("b (i p) c -> b p i c", p=P)
    adj_d = adj.rearrange("b (i p) m -> b p i m", p=P)
    out_d = out.rearrange("b (i p) c -> b p i c", p=P)

    with ExitStack() as ctx:
        def sb(name, shape, dt=F32):
            return ctx.enter_context(nc.sbuf_tensor(name, shape, dt))

        def sem(name):
            return ctx.enter_context(nc.semaphore(name))

        ident = sb("ident", [P, P])
        ones_bf = sb("ones_bf", [P, P], BF16)
        nhalf = sb("nhalf", [P, 2 * RB])
        fold = sb("fold", [P, C])
        ident_r = sb("ident_r", [P, P], F32R)
        cheb_ws = sb("cheb_ws", [P, K, C])
        cheb_hi = sb("cheb_hi", [P, K - 1, C], F32R)
        cheb_lo = sb("cheb_lo", [P, K - 1, C], F32R)
        enc_ws = sb("enc_ws", [P, H])
        enc_hi = sb("enc_hi", [P, H], F32R)
        enc_lo = sb("enc_lo", [P, H], F32R)
        att_ws = [[sb(f"att_w{a}{k}", [H, H]) for k in range(3)] for a in range(2)]
        w1_s = sb("w1_s", [H, 2, H])
        w2_s = sb("w2_s", [H, H])
        w3_s = sb("w3_s", [H, C])
        gcn_ws = sb("gcn_ws", [P, C])
        enc_bs = sb("enc_bs", [H, 1])
        kq_bs = [[None] + [sb(f"kq_b{a}{k}", [H, 1]) for k in (1, 2)] for a in range(2)]
        b1_s = sb("b1_s", [H, 1])
        b2_s = sb("b2_s", [H, 1])
        cheb_bs = sb("cheb_bs", [P, C])
        b3_s = sb("b3_s", [P, C])
        bv_f = [sb(f"bv_f{a}", [P, H]) for a in range(2)]
        bv_rows = [sb(f"bv_rows{a}", [P, RB, H], BF16) for a in range(2)]

        a_nat = [sb(f"a_nat{s}", [P, RB, N]) for s in range(SLOTS)]
        at_hi = [sb(f"at_hi{s}", [P, RB, N], F32R) for s in range(SLOTS)]
        at_lo = [sb(f"at_lo{s}", [P, RB, N], F32R) for s in range(SLOTS)]
        x_in = [sb(f"x_in{s}", [P, RB, C]) for s in range(SLOTS)]
        x_b = sb("x_b", [P, RB, C])
        x1 = [sb(f"x1_{s}", [P, RB, C]) for s in range(SLOTS)]
        x1b = [sb(f"x1b_{s}", [P, RB, C]) for s in range(SLOTS)]
        rs = sb("rs", [P, 2 * RB])
        dinv = [sb(f"dinv{s}", [P, 2 * RB]) for s in range(SLOTS)]
        h2_t = [sb(f"h2_t{s}", [P, N]) for s in range(SLOTS)]
        x_out = [sb(f"x_out{s}", [P, RB, C]) for s in range(SLOTS)]

        junk = sb("junk", [P, N], BF16)
        positive = sb("positive", [P, RB])
        d_m2 = sb("d_m2", [P, RB])
        d_neg = sb("d_neg", [P, RB])
        d_root = sb("d_root", [P, RB])
        stats = {t: sb(f"stats_{t}", [P, RB, 6]) for t in ("pre", "post")}
        meanvar = {t: sb(f"meanvar_{t}", [P, RB, 2]) for t in ("pre", "post")}
        vareps = {t: sb(f"vareps_{t}", [P, RB]) for t in ("pre", "post")}
        rstd = {t: sb(f"rstd_{t}", [P, RB]) for t in ("pre", "post")}
        rstd_d = sb("rstd_d", [P, RB])
        centred = {t: sb(f"centred_{t}", [P, RB, C]) for t in ("pre", "post")}
        h_nat = {"pre": sb("h_nat_pre", [P, RB, 2, C]), "post": sb("h_nat_post", [P, RB, C])}
        h_t = sb("h_t", [P, N], F32R)
        u_pair = {t: sb(f"u_pair_{t}", [P, RB, 2, C], F32R) for t in ("pre", "post")}
        y_t = {t: sb(f"y_t_{t}", [P, N]) for t in ("pre", "post")}
        u3 = sb("u3", [P, RB, C])
        c2 = sb("c2", [P, RB, C])
        c1 = sb("c1", [P, RB, C])
        e2 = sb("e2", [P, RB, C])
        e1 = sb("e1", [P, RB, C])
        f0 = sb("f0", [P, RB, C])
        tmp = sb("tmp", [P, RB, C])
        c_diff = sb("c_diff", [P, RB, C])
        q_t, k_t, v_n = (sb(n, [P, N]) for n in ("q_t", "k_t", "v_n"))
        q_hi, k_hi, v_hi, q_lo, k_lo, v_lo = (
            [sb(f"{n}{a}", [P, N], F32R) for a in range(2)]
            for n in ("q_hi", "k_hi", "v_hi", "q_lo", "k_lo", "v_lo"))
        h1_t = sb("h1_t", [P, N])
        h3_t = sb("h3_t", [P, N])
        gate = sb("gate", [P, RB, N])
        negz = sb("negz", [P, RB, N])
        negmax = sb("negmax", [P, RB])
        probs = negz
        total = sb("total", [P, RB])
        inv_total = sb("inv_total", [P, RB])
        pt_hi = sb("pt_hi", [P, RB, N], F32R)
        pt_lo = sb("pt_lo", [P, RB, N], F32R)
        inv_row = sb("inv_row", [P, N])
        z1_t = sb("z1_t", [P, N])
        z2_t = sb("z2_t", [P, N])
        x2 = sb("x2", [P, RB, C])
        x3 = sb("x3", [P, RB, C])
        u2 = sb("u2", [P, RB, C])
        s2 = sb("s2", [P, RB, C])
        last = s2

        def bank(name):
            return ctx.enter_context(nc.psum_tensor(name, [P, N], F32))

        score_ps = [bank(f"score_ps{k}") for k in range(2)]
        turn_ps = [bank(f"turn_ps{k}") for k in range(2)]
        qkv_ps = bank("qkv_ps")
        post_ps = bank("post_ps")
        pre_ps = ctx.enter_context(nc.psum_tensor("pre_ps", [P, 2, N], F32))

        weights_in = sem("weights_in")
        early_in = sem("early_in")
        consts_done = sem("consts_done")
        bias_rows = sem("bias_rows")
        weights_split = sem("weights_split")
        a_loaded = [sem(f"a_loaded{s}") for s in range(SLOTS)]
        x_loaded = [sem(f"x_loaded{s}") for s in range(SLOTS)]
        x_out_free = [sem(f"x_out_free{s}") for s in range(SLOTS)]
        at_ready = sem("at_ready")
        ht_ready = sem("ht_ready")
        cheb_ready = sem("cheb_ready")
        y_ready = {t: sem(f"y_ready_{t}") for t in ("pre", "post")}
        prop_ready = sem("prop_ready")
        enc_ready = sem("enc_ready")
        qk_ready = sem("qk_ready")
        v_ready = sem("v_ready")
        scores_ready = sem("scores_ready")
        pt_ready = sem("pt_ready")
        inv_ready = sem("inv_ready")
        pv_ready = sem("pv_ready")
        mlp_ready = sem("mlp_ready")
        gcn_ready = sem("gcn_ready")
        last_ready = sem("last_ready")
        rowsums = sem("rowsums")
        at_copied = sem("at_copied")
        ht_copied = sem("ht_copied")
        y_copied = {t: sem(f"y_copied_{t}") for t in ("pre", "post")}
        h1_done = sem("h1_done")
        qkv_done = sem("qkv_done")
        probs_done = sem("probs_done")
        pt_copied = sem("pt_copied")
        inv_copied = sem("inv_copied")
        z_done = sem("z_done")
        var_ready = {t: sem(f"var_ready_{t}") for t in ("pre", "post")}
        h_ready = {t: sem(f"h_ready_{t}") for t in ("pre", "post")}
        at_split = sem("at_split")
        ht_split = sem("ht_split")
        u_split = {t: sem(f"u_split_{t}") for t in ("pre", "post")}
        pt_split = sem("pt_split")
        cheb_taken = sem("cheb_taken")
        c_ready = sem("c_ready")
        x1_done = sem("x1_done")
        masked = sem("masked")
        biased = sem("biased")
        inv_done = sem("inv_done")
        attended = sem("attended")
        x2_done = sem("x2_done")
        u2_done = sem("u2_done")
        x3_done = sem("x3_done")
        out_done = sem("out_done")
        dve_pre = Chain(sem("dve_pre"), 2 * 6 + 6)
        dve_post = Chain(sem("dve_post"), 2 * 5 + 3 + 2)
        gate_done = sem("gate_done")
        xb_done = sem("xb_done")
        x1b_done = sem("x1b_done")
        dinv_done = sem("dinv_done")
        f0_done = sem("f0_done")
        qkv_split = sem("qkv_split")
        rstd_done = {t: sem(f"rstd_done_{t}") for t in ("pre", "post")}
        pool_pre = Chain(sem("pool_pre"), 7 + 4)

        def follows(g, a=0):
            return not isinstance(g.n, int) or g.n > 0 or a > 0

        def over_blocks(per_row):
            return per_row.unsqueeze(2).to_broadcast([P, RB, C])

        def over_rows(per_channel):
            return per_channel.unsqueeze(1).to_broadcast([P, RB, C])

        def rows(ps):
            return ps[:, 0:RB * C].rearrange("p (i c) -> p i c", c=C)

        def cheb_part(k):
            return pre_ps[:, :, 0:RB // 2 * (K - 1) * C]\
                .rearrange("p a (i k c) -> p a i k c", k=K - 1, c=C)[:, :, :, k, :]

        def by_bank(t):
            return t.rearrange("p (a i) c -> p a i c", a=2)

        def first(g):
            return isinstance(g.n, int) and g.n == 0

        def walk(engine, steps, chains=()):
            order = [(entry[:-2], int(entry[-1])) for entry in ORDER[engine]]
            assert sorted(name for name, _ in order) == sorted(steps), engine

            def one(*graphs):
                for chain in chains:
                    chain.next_round()
                for name, age in order:
                    g = graphs[age]
                    if g is not None:
                        for chain in chains:
                            chain.turn_to(g, age)
                        steps[name](g)
            return one

        def layer(a, **steps):
            def bind(f):
                return lambda g: f(g, a)
            return {f"{name}.{a + 1}": bind(f) for name, f in steps.items()}

        def rounds(eng, one):
            one(Graph(0, 0), None, None)
            one(Graph(0, 1), Graph(0, 0), None)
            one(Graph(0, 2), Graph(0, 1), Graph(0, 0))
            with eng.Fori(0, (B - 4) // SLOTS) as turn:
                for u in range(2, 2 + SLOTS):
                    one(Graph(turn, u + 1), Graph(turn, u), Graph(turn, u - 1))
            one(Graph(0, B - 1), Graph(0, B - 2), Graph(0, B - 3))
            one(None, Graph(0, B - 1), Graph(0, B - 2))
            one(None, None, Graph(0, B - 1))

        n_early, n_small = 6, 2 * 6 + 8
        held = sem("held")

        def hold(eng):
            eng.sem_inc(held)

        block = ctx.enter_context(nc.Block())

        @block.sync
        def _(sp):
            early = [(half, cheb_w.rearrange("k o c d -> (o c) k d"))
                     for half in (cheb_ws[0:C], cheb_ws[C:P])]
            early += [(cheb_bs[:], cheb_b.rearrange("a b c -> (a b c)").partition_broadcast(P))]
            early += [(half, enc_w) for half in (enc_ws[0:C], enc_ws[C:P])]
            early += [(enc_bs[:], enc_b.rearrange("(h o) -> h o", o=1))]
            small = []
            for a in range(2):
                small += [(att_ws[a][k][:], att_w[a][k]) for k in range(3)]
                small += [(kq_bs[a][k][:], att_b[a][k].rearrange("(h o) -> h o", o=1)) for k in (1, 2)]
                small += [(bv_f[a][:], att_b[a][0].partition_broadcast(P))]
            small += [(w1_s[:], w1.rearrange("(a h) n -> h a n", a=2)), (w2_s[:], w2), (w3_s[:], w3),
                      (b1_s[:], b1.rearrange("(h o) -> h o", o=1)),
                      (b2_s[:], b2.rearrange("(h o) -> h o", o=1)),
                      (b3_s[:], b3.partition_broadcast(P))]
            small += [(half, gcn_w) for half in (gcn_ws[0:C], gcn_ws[C:P])]
            assert len(early) == n_early and len(small) == n_small

            def load(g, waits=True):
                if waits:
                    sp.wait_ge(biased, 8 * (g.n - SLOTS) + 8)
                    hold(sp)
                    sp.wait_ge(x1_done, g.n - SLOTS + 1)
                sp.dma_start(x_in[g.slot][:], x_d[g.n]).then_inc(x_loaded[g.slot], 16)
                sp.dma_start(a_nat[g.slot][:], adj_d[g.n]).then_inc(a_loaded[g.slot], 16)

            def store(g):
                sp.wait_ge(out_done, g.n + 1)
                sp.dma_start(out_d[g.n], x_out[g.slot][:]).then_inc(x_out_free[g.slot], 16)

            load(Graph(0, 0), False)
            for s in range(SLOTS):
                sp.sem_inc(x_out_free[s])
            for to, what in early:
                sp.dma_start(to, what).then_inc(early_in, 16)
            for to, what in small:
                sp.dma_start(to, what).then_inc(weights_in, 16)
            load(Graph(0, 1), False)
            load(Graph(0, 2), False)
            load(Graph(0, 3))
            store(Graph(0, 0))
            with sp.Fori(0, (B - 4) // SLOTS) as turn:
                for u in range(2, 2 + SLOTS):
                    load(Graph(turn, u + 2))
                    store(Graph(turn, u - 1))
            for n in range(B - 3, B):
                store(Graph(0, n))
            for s in range(SLOTS):
                sp.wait_ge(x_out_free[s], 1 + 16 * len(range(s, B, SLOTS)))

        n_bias_rows = 2 * (3 + 2 + 1 + 2 + 1 + RB - 1)

        @block.gpsimd
        def _(pool):
            gp = nc.gpsimd
            gp.memset(ident[:], 0.0).then_inc(consts_done, 1)
            gp.memset(ones_bf[:], 1.0).then_inc(consts_done, 1)
            gp.memset(nhalf[:], -0.5).then_inc(consts_done, 1)
            for a in range(2):
                gp.memset(bv_rows[a][:], 0.0).then_inc(consts_done, 1)
            pool.wait_ge(consts_done, 5)
            gp.affine_select(out=ident[:], in_=ident[:], compare_op=ALU.not_equal, fill=1.0, base=0,
                             pattern=[[-1, P]], channel_multiplier=1).then_inc(consts_done, 1)
            pool.wait_ge(consts_done, 6)
            gp.tensor_tensor(fold[:], ident[:, 0:C], ident[:, C:P], ALU.add).then_inc(consts_done, 1)

            def scale_norm(t, k):
                def f(g):
                    pool.wait_ge(var_ready[t], 2 * g.n + k + 1)
                    gp.tensor_tensor(rstd[t][:], vareps[t][:], nhalf[:, 0:RB], ALU.pow)\
                        .then_inc(rstd_done[t], 1)
                    src = {"pre": (x_in[g.slot], x1[g.slot]), "post": (x2, x3)}[t][k]
                    gp.tensor_tensor(centred[t][:], src[:], meanvar[t][:, :, 0:1].to_broadcast([P, RB, C]),
                                     ALU.subtract).then_inc(rstd_done[t], 1)
                return f

            def add_cheb_bias(g):
                pool.wait_ge(x_loaded[g.slot], 16 * (g.round + 1))
                if first(g):
                    pool.wait_ge(early_in, 16 * n_early)
                if follows(g):
                    pool.wait_ge(x1_done, g.n)
                gp.tensor_tensor(x_b[:], x_in[g.slot][:], over_rows(cheb_bs[:]), ALU.add)\
                    .then_inc(xb_done, 1)

            def inverse_roots(g):
                pool.wait_ge(rowsums, 4 * g.n + 4)
                if not isinstance(g.n, int) or g.n >= SLOTS:
                    hold(pool)
                    pool.wait_ge(x3_done, g.n - SLOTS + 1)
                hold(pool)
                d = dinv[g.slot]
                pool_pre.add(gp.tensor_scalar(rs[:, RB:], rs[:, 0:RB], 1.0, TINY, ALU.add, ALU.max))
                pool_pre.add(gp.tensor_scalar(positive[:], rs[:, 0:RB], 1.0, 0.0, ALU.add, ALU.is_gt))
                pool.wait_ge(pool_pre.sem, pool_pre.so_far())
                pool_pre.add(gp.tensor_tensor(d[:], rs[:], nhalf[:], ALU.pow))
                pool.wait_ge(pool_pre.sem, pool_pre.so_far())
                pool_pre.add(gp.tensor_tensor(d[:, RB:], d[:, RB:], positive[:], ALU.mult))
                pool_pre.add(gp.tensor_scalar(d_neg[:], d[:, 0:RB], -1.0, None, ALU.mult))
                pool_pre.add(gp.tensor_tensor(d_root[:], d[:, 0:RB], rs[:, 0:RB], ALU.mult))
                pool_pre.add(gp.tensor_scalar(d_m2[:], d[:, 0:RB], -2.0, None, ALU.mult))
                pool.wait_ge(pool_pre.sem, pool_pre.so_far())
                gp.tensor_tensor(d_m2[:], d_m2[:], d[:, 0:RB], ALU.mult).then_inc(dinv_done, 1)

            def cheb_u3(g):
                pool.wait_ge(h_ready["pre"], 2 * g.n + 1)
                pool.wait_ge(dinv_done, g.n + 1)
                pool_pre.add(gp.tensor_tensor(u3[:], h_nat["pre"][:, :, 0, :],
                                              over_blocks(dinv[g.slot][:, 0:RB]), ALU.mult))
                if follows(g):
                    pool.wait_ge(y_ready["pre"], 3 * g.n)
                pool.wait_ge(pool_pre.sem, pool_pre.so_far())
                hold(pool)
                pool_pre.add(gp.tensor_copy(u_pair["pre"][:, :, 0, :], u3[:]))
                pool.wait_ge(pool_pre.sem, pool_pre.so_far())
                gp.tensor_tensor(u_pair["pre"][:, :, 1, :], u3[:],
                                 u_pair["pre"][:, :, 0, :].bitcast(F32),
                                 ALU.subtract).then_inc(u_split["pre"], 1)

            def cheb_f0(g):
                pool.wait_ge(c_ready, 2 * g.n + 2)
                pool_pre.add(gp.tensor_tensor(c_diff[:], c1[:], c2[:], ALU.subtract))
                pool.wait_ge(pool_pre.sem, pool_pre.so_far())
                pool_pre.add(gp.tensor_tensor(c_diff[:], c_diff[:], over_blocks(d_root[:]), ALU.mult))
                pool.wait_ge(cheb_taken, 3 * g.n + 3)
                pool.wait_ge(pool_pre.sem, pool_pre.so_far())
                gp.tensor_tensor(f0[:], f0[:], c_diff[:], ALU.add).then_inc(f0_done, 1)

            def mask_bias(g, a):
                if follows(g, a):
                    pool.wait_ge(biased, 8 * g.n + 4 * a)
                    hold(pool)
                gp.tensor_scalar(gate[:], a_nat[g.slot][:], -1.0, NEG, ALU.add, ALU.mult)\
                    .then_inc(gate_done, 1)

            def split(whole, high, low, g, a, k):
                pool.wait_ge(qkv_done, 12 * g.n + 6 * a + 2 * k + 2)
                gp.tensor_tensor(low[a][:], whole[:], high[a][:].bitcast(F32), ALU.subtract)\
                    .then_inc(qkv_split, 1)

            def queries_keys(g, a):
                split(q_t, q_hi, q_lo, g, a, 0)
                split(k_t, k_hi, k_lo, g, a, 1)

            def values(g, a):
                split(v_n, v_hi, v_lo, g, a, 2)

            def add_mlp_bias(g):
                if first(g):
                    pool.wait_ge(weights_in, 16 * n_small)
                pool.wait_ge(x1_done, g.n + 1)
                if not isinstance(g.n, int) or g.n >= SLOTS:
                    hold(pool)
                    pool.wait_ge(x2_done, g.n - SLOTS + 1)
                gp.tensor_tensor(x1b[g.slot][:], x1[g.slot][:], over_rows(b3_s[:]), ALU.add)\
                    .then_inc(x1b_done, 1)

            rounds(pool, walk("gpsimd", {
                "norm_cheb": scale_norm("pre", 0), "add_cheb_bias": add_cheb_bias,
                "inverse_roots": inverse_roots, "cheb_u3": cheb_u3, "cheb_f0": cheb_f0, "norm_enc": scale_norm("pre", 1),
                "add_mlp_bias": add_mlp_bias,
                **layer(0, split_qk=queries_keys, split_v=values, mask_bias=mask_bias),
                **layer(1, split_qk=queries_keys, split_v=values),
                **layer(1, mask_bias=mask_bias),
                "norm_gcn": scale_norm("post", 0), "norm_last": scale_norm("post", 1),
            }, (pool_pre,)))

        @block.scalar
        def _(act):
            sc = nc.scalar

            def copy_at(j):
                def f(g):
                    act.wait_ge(at_ready, 4 * g.n + j + 1)
                    sc.activation(at_hi[g.slot][:, j, :], pre_ps[:, j % 2, :], ACT.Copy)\
                        .then_inc(at_copied, 1)
                return f

            def row_sum(i):
                def f(g):
                    if i == 0:
                        act.wait_ge(a_loaded[g.slot], 16 * (g.round + 1))
                        if follows(g):
                            act.wait_ge(dinv_done, g.n)
                    if i or follows(g):
                        act.wait_ge(rowsums, 4 * g.n + i)
                    sc.activation(junk[:], a_nat[g.slot][:, i, :], ACT.Copy,
                                  accum_out=rs[:, i:i + 1]).then_inc(rowsums, 1)
                return f

            def copy_ht(k):
                def f(g):
                    act.wait_ge(ht_ready, 2 * g.n + k + 1)
                    sc.activation(h_t[:], pre_ps[:, 0, :], ACT.Copy).then_inc(ht_copied, 1)
                return f

            def copy_y(t, k, per, ps):
                def f(g):
                    act.wait_ge(y_ready[t], per * g.n + k + 1)
                    sc.activation(y_t[t][:], ps, ACT.Copy).then_inc(y_copied[t], 1)
                return f

            def encode(g):
                if first(g):
                    act.wait_ge(early_in, 16 * n_early)
                act.wait_ge(enc_ready, g.n + 1)
                if follows(g):
                    act.wait_ge(v_ready, 2 * g.n - 1)
                sc.activation(h1_t[:], pre_ps[:, 1, :], ACT.Tanh, bias=enc_bs[:])\
                    .then_inc(h1_done, 1)

            def take(g, a, k, whole, high, bias):
                for n, to in enumerate((high[a], whole)):
                    if n and follows(g, a):
                        act.wait_ge(qkv_split, 6 * g.n + 3 * a + k - 2)
                    sc.activation(to[:], qkv_ps[:], ACT.Tanh, **bias).then_inc(qkv_done, 1)

            def queries(g, a):
                if first(g) and a == 0:
                    act.wait_ge(weights_in, 16 * n_small)
                act.wait_ge(qk_ready, 4 * g.n + 2 * a + 1)
                take(g, a, 0, q_t, q_hi, {"bias": kq_bs[a][2][:]})

            def keys(g, a):
                act.wait_ge(qk_ready, 4 * g.n + 2 * a + 2)
                take(g, a, 1, k_t, k_hi, {"bias": kq_bs[a][1][:]})

            def values(g, a):
                act.wait_ge(v_ready, 2 * g.n + a + 1)
                take(g, a, 2, v_n, v_hi, {})

            def exponent(i):
                def f(g, a):
                    if i == 0 and follows(g, a):
                        act.wait_ge(inv_done, 2 * g.n + a)
                    act.wait_ge(biased, 8 * g.n + 4 * a + i + 1)
                    sc.activation(probs[:, i, :], negz[:, i, :], ACT.Exp, bias=negmax[:, i:i + 1],
                                  scale=-1.0, accum_out=total[:, i:i + 1]).then_inc(probs_done, 1)
                return f

            def copy_pt(i):
                def f(g, a):
                    act.wait_ge(pt_ready, 8 * g.n + 4 * a + i + 1)
                    sc.activation(pt_hi[:, :, i * P:(i + 1) * P],
                                  turn_ps[i % 2][:].rearrange("p (j n) -> p j n", n=P), ACT.Copy)\
                        .then_inc(pt_copied, 1)
                return f

            def copy_inv(g, a):
                act.wait_ge(inv_ready, 2 * g.n + a + 1)
                sc.activation(inv_row[:], turn_ps[1][:], ACT.Copy).then_inc(inv_copied, 1)

            def mlp(k, to, ps, bias):
                def f(g):
                    act.wait_ge(mlp_ready, 3 * g.n + k + 1)
                    sc.activation(to[:], ps[:], ACT.Relu, bias=bias[:]).then_inc(z_done, 1)
                return f

            rounds(act, walk("scalar", {
                "copy_at0": copy_at(0), "row_sum0": row_sum(0), "copy_at1": copy_at(1),
                "row_sum1": row_sum(1), "copy_at2": copy_at(2), "row_sum2": row_sum(2),
                "copy_at3": copy_at(3), "row_sum3": row_sum(3),
                "cheb_ht": copy_ht(0),
                "cheb_copy3": copy_y("pre", 0, 3, pre_ps[:, 0, :]),
                "cheb_copy2": copy_y("pre", 1, 3, pre_ps[:, 0, :]),
                "cheb_copy1": copy_y("pre", 2, 3, pre_ps[:, 0, :]),
                "enc_ht": copy_ht(1),
                "encode": encode,
                **layer(0, queries=queries, keys=keys, values=values, exp0=exponent(0),
                    exp1=exponent(1), copy_pt0=copy_pt(0), exp2=exponent(2),
                    copy_pt1=copy_pt(1), exp3=exponent(3), copy_pt2=copy_pt(2),
                    copy_pt3=copy_pt(3), copy_inv=copy_inv),
                **layer(1, queries=queries, keys=keys, values=values),
                **layer(1, exp0=exponent(0), exp1=exponent(1), copy_pt0=copy_pt(0),
                    exp2=exponent(2), copy_pt1=copy_pt(1), exp3=exponent(3),
                    copy_pt2=copy_pt(2), copy_pt3=copy_pt(3), copy_inv=copy_inv),
                "mlp1": mlp(0, z1_t, post_ps, b1_s), "mlp2": mlp(1, z2_t, post_ps, b2_s),
                "gcn_copy": copy_y("post", 0, 2, post_ps[:]),
                "last_copy": copy_y("post", 1, 2, post_ps[:]),
            }))

        @block.vector
        def _(dve):
            ve = nc.vector

            def set_bias_rows():
                dve.wait_ge(weights_in, 16 * n_small)
                made = 0
                for a in range(2):
                    rest = bv_f[a]
                    for row, p0 in enumerate((0, 32, 64)):
                        for p1 in range(p0, 96, 32):
                            ve.tensor_copy(bv_rows[a][p1:p1 + 1, 0, :], rest[p1:p1 + 1, :])\
                                .then_inc(bias_rows, 1)
                            made += 1
                        dve.wait_ge(bias_rows, made)
                        for p1 in range(p0 + 32, 96, 32):
                            ve.tensor_tensor(rest[p1:p1 + 1, :], rest[p1:p1 + 1, :],
                                             bv_rows[a][p1:p1 + 1, 0, :], ALU.subtract)\
                                .then_inc(bias_rows, 1)
                            made += 1
                        dve.wait_ge(bias_rows, made)
                    for i in range(1, RB):
                        ve.tensor_copy(bv_rows[a][0:96, i, :], bv_rows[a][0:96, 0, :])\
                            .then_inc(bias_rows, 1)
                        made += 1
                assert made == n_bias_rows

            dve.wait_ge(consts_done, 7)
            ve.tensor_copy(ident_r[:], ident[:]).then_inc(weights_split, 1)
            dve.wait_ge(early_in, 16 * n_early)
            ve.scalar_tensor_tensor(cheb_ws[:, 2, :], cheb_ws[:, 3, :], 2.0, cheb_ws[:, 2, :],
                                    ALU.mult, ALU.add).then_inc(weights_split, 1)
            ve.tensor_tensor(cheb_ws[:, 1, :], cheb_ws[:, 1, :], cheb_ws[:, 3, :], ALU.subtract)\
                .then_inc(weights_split, 1)
            dve.wait_ge(weights_split, 3)
            splits = ((cheb_ws[:, 0:K - 1, :], cheb_hi, cheb_lo), (enc_ws[:], enc_hi, enc_lo))
            for whole, high, low in splits:
                ve.tensor_copy(high[:], whole).then_inc(weights_split, 1)
            dve.wait_ge(weights_split, 5)
            for whole, high, low in splits:
                ve.tensor_tensor(low[:], whole, high[:].bitcast(F32), ALU.subtract)\
                    .then_inc(weights_split, 1)

            def norm_stats(t, chain, g, k, src):
                st, mv = stats[t], meanvar[t]
                for i in range(RB):
                    chain.add(ve.bn_stats(st[:, i, :], src[:, i, :]))
                dve.wait_ge(chain.sem, chain.so_far())
                hold(dve)
                for i in range(RB):
                    last_one = ve.bn_aggr(mv[:, i, :], st[:, i, :])
                chain.add(last_one)
                dve.wait_ge(chain.sem, chain.so_far())
                ve.tensor_scalar(vareps[t][:], mv[:, :, 1], EPS, None, ALU.add)\
                    .then_inc(var_ready[t], 1)

            def norm_apply(t, chain, g, k):
                dve.wait_ge(rstd_done[t], 4 * g.n + 2 * k + 2)
                to = h_nat[t][:, :, 0, :] if t == "pre" else h_nat[t][:]
                one = ve.scalar_tensor_tensor(to, centred[t][:], 0.0, over_blocks(rstd[t][:]),
                                              ALU.max, ALU.mult)
                if t == "post":
                    one.then_inc(h_ready[t], 1)
                    return
                chain.add(one)
                dve.wait_ge(chain.sem, chain.so_far())
                ve.tensor_copy(h_nat[t][:, :, 1, :], to).then_inc(h_ready[t], 1)

            def split_at(j):
                def f(g):
                    dve.wait_ge(at_copied, 4 * g.n + j + 1)
                    ve.tensor_tensor(at_lo[g.slot][:, j, :], pre_ps[:, j % 2, :],
                                     at_hi[g.slot][:, j, :].bitcast(F32), ALU.subtract)\
                        .then_inc(at_split, 1)
                return f

            def split_ht(g, k):
                dve.wait_ge(ht_copied, 2 * g.n + k + 1)
                ve.tensor_tensor(h_t[C:P, :], pre_ps[C:P, 0, :], h_t[C:P, :].bitcast(F32),
                                 ALU.subtract).then_inc(ht_split, 1)
                if first(g) and k == 1:
                    set_bias_rows()

            def split_u(t, chain, u):
                chain.add(ve.tensor_copy(u_pair[t][:, :, 0, :], u[:]))
                dve.wait_ge(chain.sem, chain.so_far())
                ve.tensor_tensor(u_pair[t][:, :, 1, :], u[:], u_pair[t][:, :, 0, :].bitcast(F32),
                                 ALU.subtract).then_inc(u_split[t], 1)

            def stats_cheb(g):
                dve.wait_ge(x_loaded[g.slot], 16 * (g.round + 1))
                norm_stats("pre", dve_pre, g, 0, x_in[g.slot])

            def cheb_norm(g):
                if follows(g):
                    dve.wait_ge(ht_ready, 2 * g.n)
                norm_apply("pre", dve_pre, g, 0)

            def cheb_weights(g):
                d = by_bank(over_blocks(dinv[g.slot][:, 0:RB]))
                dve.wait_ge(cheb_ready, g.n + 1)
                dve.wait_ge(dinv_done, g.n + 1)
                ve.tensor_tensor(by_bank(e2[:]), cheb_part(2), d, ALU.mult).then_inc(cheb_taken, 1)
                ve.tensor_tensor(by_bank(e1[:]), cheb_part(1), d, ALU.mult).then_inc(cheb_taken, 1)
                dve.wait_ge(xb_done, g.n + 1)
                ve.tensor_tensor(by_bank(f0[:]), cheb_part(0), by_bank(x_b[:]), ALU.add)\
                    .then_inc(cheb_taken, 1)

            def cheb_fold3(g):
                dve.wait_ge(prop_ready, 3 * g.n + 1)
                dve_pre.add(ve.tensor_tensor(tmp[:], rows(pre_ps[:, 1, :]), over_blocks(d_m2[:]), ALU.mult))
                dve.wait_ge(dve_pre.sem, dve_pre.so_far())
                dve.wait_ge(cheb_taken, 3 * g.n + 2)
                ve.tensor_tensor(c2[:], tmp[:], e2[:], ALU.add).then_inc(c_ready, 1)
                dve.wait_ge(c_ready, 2 * g.n + 1)
                split_u("pre", dve_pre, c2)
                dve_pre.add(ve.scalar_tensor_tensor(e1[:], c2[:], 2.0, e1[:], ALU.mult, ALU.add))

            def cheb_fold2(g):
                dve.wait_ge(prop_ready, 3 * g.n + 2)
                dve_pre.add(ve.tensor_tensor(tmp[:], rows(pre_ps[:, 1, :]), over_blocks(d_m2[:]), ALU.mult))
                dve.wait_ge(dve_pre.sem, dve_pre.so_far())
                ve.tensor_tensor(c1[:], tmp[:], e1[:], ALU.add).then_inc(c_ready, 1)
                dve.wait_ge(c_ready, 2 * g.n + 2)
                split_u("pre", dve_pre, c1)

            def cheb_fold1(g):
                dve.wait_ge(prop_ready, 3 * g.n + 3)
                dve.wait_ge(f0_done, g.n + 1)
                dve.wait_ge(dve_pre.sem, dve_pre.so_far())
                dve_pre.add(ve.tensor_tensor(tmp[:], rows(pre_ps[:, 1, :]), over_blocks(d_neg[:]), ALU.mult))
                dve.wait_ge(dve_pre.sem, dve_pre.so_far())
                ve.tensor_tensor(x1[g.slot][:], tmp[:], f0[:], ALU.add).then_inc(x1_done, 1)

            def stats_enc(g):
                dve.wait_ge(x1_done, g.n + 1)
                norm_stats("pre", dve_pre, g, 1, x1[g.slot])

            def enc_norm(g):
                norm_apply("pre", dve_pre, g, 1)

            def mask(i):
                return lambda g, a: mask_rows(g, a, i)

            def mask_rows(g, a, i):
                n = 4 * a + i
                s = g.slot
                if follows(g, a):
                    dve.wait_ge(pt_ready, 8 * g.n + n - 3)
                dve.wait_ge(scores_ready, 8 * g.n + n + 1)
                ve.tensor_tensor(negz[:, i, :], score_ps[i % 2][:], a_nat[s][:, i, :], ALU.mult)\
                    .then_inc(masked, 1)
                if i == 0:
                    dve.wait_ge(gate_done, 2 * g.n + a + 1)
                dve.wait_ge(masked, 8 * g.n + n + 1)
                hold(dve)
                ve.tensor_tensor_reduce(negz[:, i, :], negz[:, i, :], gate[:, i, :], -1.0, 3.0e38,
                                        ALU.add, ALU.min, negmax[:, i:i + 1]).then_inc(biased, 1)

            def split_pt(i):
                return lambda g, a: split_rows(g, a, i)

            def split_rows(g, a, i):
                dve.wait_ge(pt_copied, 8 * g.n + 4 * a + i + 1)
                part = slice(i * P, (i + 1) * P)
                ve.tensor_tensor(pt_lo[:, :, part], turn_ps[i % 2][:].rearrange("p (j n) -> p j n", n=P),
                                 pt_hi[:, :, part].bitcast(F32), ALU.subtract).then_inc(pt_split, 1)

            def invert(g, a):
                dve.wait_ge(probs_done, 8 * g.n + 4 * a + 4)
                ve.reciprocal(inv_total[:], total[:]).then_inc(inv_done, 1)

            def attend(g, a):
                to = h3_t if a else h2_t[g.slot]
                dve.wait_ge(inv_copied, 2 * g.n + a + 1)
                dve.wait_ge(pv_ready, 2 * g.n + a + 1)
                ve.tensor_tensor(to[:], turn_ps[0][:], inv_row[:], ALU.mult).then_inc(attended, 1)

            def mlp3(g):
                dve.wait_ge(mlp_ready, 3 * g.n + 3)
                dve.wait_ge(x1b_done, g.n + 1)
                ve.tensor_tensor(x2[:], rows(post_ps[:]), x1b[g.slot][:], ALU.add).then_inc(x2_done, 1)

            def stats_gcn(g):
                dve.wait_ge(x2_done, g.n + 1)
                norm_stats("post", dve_post, g, 0, x2)

            def gcn_norm(g):
                dve.wait_ge(rstd_done["post"], 4 * g.n + 2)
                dve_post.add(ve.tensor_tensor(rstd_d[:], rstd["post"][:], dinv[g.slot][:, RB:],
                                              ALU.mult))
                dve.wait_ge(dve_post.sem, dve_post.so_far())
                ve.scalar_tensor_tensor(u2[:], centred["post"][:], 0.0, over_blocks(rstd_d[:]),
                                        ALU.max, ALU.mult).then_inc(u2_done, 1)
                dve.wait_ge(u2_done, g.n + 1)
                split_u("post", dve_post, u2)

            def gcn_fold(g):
                dve.wait_ge(gcn_ready, g.n + 1)
                dve_post.add(ve.tensor_tensor(s2[:], rows(post_ps[:]),
                                              over_blocks(dinv[g.slot][:, RB:]), ALU.mult))
                dve.wait_ge(dve_post.sem, dve_post.so_far())
                ve.scalar_tensor_tensor(x3[:], s2[:], 0.0, x2[:], ALU.max, ALU.add).then_inc(x3_done, 1)

            def stats_last(g):
                dve.wait_ge(x3_done, g.n + 1)
                norm_stats("post", dve_post, g, 1, x3)

            def last_norm(g):
                norm_apply("post", dve_post, g, 1)
                dve.wait_ge(h_ready["post"], g.n + 1)
                split_u("post", dve_post, h_nat["post"])

            def last_fold(g):
                dve.wait_ge(last_ready, g.n + 1)
                dve_post.add(ve.scalar_tensor_tensor(last[:], rows(post_ps[:]), 0.5, x3[:],
                                                     ALU.is_gt, ALU.add))
                dve.wait_ge(dve_post.sem, dve_post.so_far())
                dve.wait_ge(x_out_free[g.slot], 1 + 16 * g.round)
                ve.scalar_tensor_tensor(x_out[g.slot][:], rows(post_ps[:]), 0.0, last[:],
                                        ALU.mult, ALU.add).then_inc(out_done, 1)

            rounds(dve, walk("vector", {
                "stats_cheb": stats_cheb, "norm_cheb": cheb_norm,
                "split_at0": split_at(0),
                "split_at1": split_at(1), "split_at2": split_at(2), "split_at3": split_at(3),
                "cheb_ht": lambda g: split_ht(g, 0),
                "cheb_weights": cheb_weights, "cheb_fold3": cheb_fold3,
                "cheb_fold2": cheb_fold2, "cheb_fold1": cheb_fold1,
                "stats_enc": stats_enc, "norm_enc": enc_norm,
                "enc_ht": lambda g: split_ht(g, 1),
                **layer(0, mask0=mask(0), mask1=mask(1), mask2=mask(2), split_pt0=split_pt(0),
                    mask3=mask(3), split_pt1=split_pt(1), split_pt2=split_pt(2),
                    invert=invert, split_pt3=split_pt(3), attend=attend),
                **layer(1, mask0=mask(0), mask1=mask(1), mask2=mask(2), split_pt0=split_pt(0),
                    mask3=mask(3), split_pt1=split_pt(1), split_pt2=split_pt(2),
                    invert=invert, split_pt3=split_pt(3), attend=attend),
                "mlp3": mlp3, "stats_gcn": stats_gcn, "norm_gcn": gcn_norm,
                "gcn_fold": gcn_fold,
                "stats_last": stats_last, "norm_last": last_norm, "last_fold": last_fold,
            }, (dve_pre, dve_post)))

        @block.tensor
        def _(pe):
            te = nc.tensor
            pe.wait_ge(consts_done, 7)

            def turn_a(j):
                def f(g):
                    pe.wait_ge(a_loaded[g.slot], 16 * (g.round + 1))
                    if j == 0 and follows(g):
                        pe.wait_ge(h1_done, g.n)
                    if j >= 2:
                        pe.wait_ge(at_split, 4 * g.n + j - 1)
                    for i in range(RB):
                        mm = te.transpose(pre_ps[:, j % 2, i * P:(i + 1) * P],
                                          a_nat[g.slot][:, i, j * P:(j + 1) * P], ident[:])
                    mm.then_inc(at_ready, 1)
                return f

            def turn_h(ready):
                pe.wait_ge(h_ready["pre"], ready)
                hold(pe)
                for i in range(RB):
                    mm = te.transpose(pre_ps[:, 0, i * P:(i + 1) * P],
                                      h_nat["pre"][:, i, :, :].rearrange("p a c -> p (a c)"), ident[:])
                mm.then_inc(ht_ready, 1)

            def cheb_ht(g):
                pe.wait_ge(at_split, 4 * g.n + 3)
                turn_h(2 * g.n + 1)

            def cheb_weights(g):
                pe.wait_ge(at_split, 4 * g.n + 4)
                pe.wait_ge(ht_split, 2 * g.n + 1)
                if first(g):
                    pe.wait_ge(weights_split, 7)
                for i in range(RB):
                    w = (K - 1) * C
                    for part in (cheb_hi, cheb_lo):
                        mm = te.matmul(pre_ps[:, i // 2, i % 2 * w:(i % 2 + 1) * w],
                                       h_t[:, i * P:(i + 1) * P],
                                       part[:].rearrange("c k d -> c (k d)"),
                                       start=(part is cheb_hi), stop=(part is cheb_lo))
                mm.then_inc(cheb_ready, 1)

            def propagate(t, g, ready, bank, own=False):
                pe.wait_ge(u_split[t], ready)
                for j in range(RB):
                    for at in (at_hi, at_lo):
                        mm = te.matmul(bank, u_pair[t][:, j, :, :].rearrange("p a c -> p (a c)"),
                                       at[g.slot][:, j, :],
                                       start=(j == 0 and at is at_hi),
                                       stop=(j == RB - 1 and at is at_lo and not own),
                                       skip_group_check=own)
                if own:
                    for j in range(RB):
                        mm = te.matmul(bank[:, j * P:(j + 1) * P],
                                       u_pair[t][:, j, :, :].rearrange("p a c -> p (a c)"), ident_r[:],
                                       start=False, stop=(j == RB - 1), skip_group_check=True)
                mm.then_inc(y_ready[t], 1)

            def fold_up(t, ready, bank, by=fold):
                pe.wait_ge(y_copied[t], ready)
                for i in range(RB):
                    mm = te.matmul(bank[:, i * C:(i + 1) * C], y_t[t][:, i * P:(i + 1) * P],
                                   by[:], start=True, stop=True)
                return mm

            def cheb_prop3(g):
                pe.wait_ge(cheb_taken, 3 * g.n + 3)
                propagate("pre", g, 3 * g.n + 1, pre_ps[:, 0, :])

            def cheb_prop(k):
                return lambda g: propagate("pre", g, 3 * g.n + k, pre_ps[:, 0, :])

            def cheb_fold(k):
                by = cheb_ws[:, K - 1, :] if k == 1 else fold
                return lambda g: fold_up("pre", 3 * g.n + k, pre_ps[:, 1, :], by).then_inc(prop_ready, 1)

            def enc_ht(g):
                turn_h(2 * g.n + 2)

            def encode(g):
                pe.wait_ge(ht_split, 2 * g.n + 2)
                te.matmul(pre_ps[:, 1, :], enc_hi[:], h_t[:], start=True, stop=False)
                te.matmul(pre_ps[:, 1, :], enc_lo[:], h_t[:], start=False, stop=True)\
                    .then_inc(enc_ready, 1)

            def source(g, a):
                return h2_t[g.slot] if a else h1_t

            def queries(g, a):
                if first(g) and a == 0:
                    pe.wait_ge(weights_in, 16 * n_small)
                if a == 0:
                    pe.wait_ge(h1_done, g.n + 1)
                else:
                    pe.wait_ge(attended, 2 * g.n + 1)
                if follows(g, a):
                    pe.wait_ge(qkv_done, 12 * g.n + 6 * a)
                te.matmul(qkv_ps[:], att_ws[a][2][:], source(g, a)[:], start=True, stop=True)\
                    .then_inc(qk_ready, 1)

            def keys(g, a):
                pe.wait_ge(qkv_done, 12 * g.n + 6 * a + 2)
                te.matmul(qkv_ps[:], att_ws[a][1][:], source(g, a)[:], start=True, stop=True)\
                    .then_inc(qk_ready, 1)

            def values(g, a):
                if first(g) and a == 0:
                    pe.wait_ge(bias_rows, n_bias_rows)
                pe.wait_ge(qkv_done, 12 * g.n + 6 * a + 4)
                te.matmul(qkv_ps[:], ones_bf[:, :],
                          bv_rows[a][:].rearrange("p i h -> p (i h)"), start=True, stop=False,
                          skip_group_check=True)
                for i in range(RB):
                    mm = te.matmul(qkv_ps[:, i * P:(i + 1) * P],
                                   source(g, a)[:, i * P:(i + 1) * P], att_ws[a][0][:],
                                   start=False, stop=(i == RB - 1), skip_group_check=True)
                mm.then_inc(v_ready, 1)

            def scores(i):
                return lambda g, a: scores_rows(g, a, i)

            def scores_rows(g, a, i):
                if i >= 2 or follows(g, a):
                    pe.wait_ge(masked, 8 * g.n + 4 * a + i - 1)
                part = slice(i * P, (i + 1) * P)
                if i == 0:
                    pe.wait_ge(qkv_done, 12 * g.n + 6 * a + 3)
                te.matmul(score_ps[i % 2][:], q_hi[a][:, part], k_hi[a][:], start=True, stop=False)
                if i == 0:
                    pe.wait_ge(qkv_split, 6 * g.n + 3 * a + 2)
                te.matmul(score_ps[i % 2][:], q_hi[a][:, part], k_lo[a][:], start=False, stop=False)
                te.matmul(score_ps[i % 2][:], q_lo[a][:, part], k_hi[a][:], start=False, stop=True)\
                    .then_inc(scores_ready, 1)

            def turn_probs(i):
                return lambda g, a: turn_rows(g, a, i)

            def turn_rows(g, a, i):
                pe.wait_ge(probs_done, 8 * g.n + 4 * a + i + 1)
                if i == 0 and follows(g, a):
                    pe.wait_ge(attended, 2 * g.n + a)
                if i >= 2:
                    pe.wait_ge(pt_split, 8 * g.n + 4 * a + i - 1)
                for j in range(RB):
                    mm = te.transpose(turn_ps[i % 2][:, j * P:(j + 1) * P],
                                      probs[:, i, j * P:(j + 1) * P], ident[:])
                mm.then_inc(pt_ready, 1)

            def spread_inv(g, a):
                pe.wait_ge(inv_done, 2 * g.n + a + 1)
                pe.wait_ge(pt_split, 8 * g.n + 4 * a + 4)
                for i in range(RB):
                    mm = te.transpose(turn_ps[1][:, i * P:(i + 1) * P],
                                      inv_total[:, i:i + 1].to_broadcast([P, P]), ident[:])
                mm.then_inc(inv_ready, 1)

            def attend(g, a):
                pe.wait_ge(qkv_split, 6 * g.n + 3 * a + 3)
                pe.wait_ge(pt_split, 8 * g.n + 4 * a + 4)
                for j in range(RB):
                    part = slice(j * P, (j + 1) * P)
                    te.matmul(turn_ps[0][:], v_hi[a][:, part], pt_hi[:, j, :], start=(j == 0), stop=False)
                    te.matmul(turn_ps[0][:], v_hi[a][:, part], pt_lo[:, j, :], start=False, stop=False)
                    mm = te.matmul(turn_ps[0][:], v_lo[a][:, part], pt_hi[:, j, :],
                                   start=False, stop=(j == RB - 1))
                mm.then_inc(pv_ready, 1)

            def mlp1(g):
                pe.wait_ge(attended, 2 * g.n + 2)
                if follows(g):
                    pe.wait_ge(out_done, g.n)
                te.matmul(post_ps[:], w1_s[:, 0, :], h2_t[g.slot][:], start=True, stop=False)
                te.matmul(post_ps[:], w1_s[:, 1, :], h3_t[:], start=False, stop=True)\
                    .then_inc(mlp_ready, 1)

            def mlp2(g):
                pe.wait_ge(z_done, 2 * g.n + 1)
                te.matmul(post_ps[:], w2_s[:], z1_t[:], start=True, stop=True)\
                    .then_inc(mlp_ready, 1)

            def mlp3(g):
                pe.wait_ge(z_done, 2 * g.n + 2)
                for i in range(RB):
                    mm = te.matmul(post_ps[:, i * C:(i + 1) * C], z2_t[:, i * P:(i + 1) * P],
                                   w3_s[:], start=True, stop=True)
                mm.then_inc(mlp_ready, 1)

            def gcn_prop(g):
                propagate("post", g, 2 * g.n + 1, post_ps[:], own=True)

            def gcn_fold(g):
                fold_up("post", 2 * g.n + 1, post_ps, gcn_ws).then_inc(gcn_ready, 1)

            def last_prop(g):
                propagate("post", g, 2 * g.n + 2, post_ps[:])

            def last_fold(g):
                fold_up("post", 2 * g.n + 2, post_ps).then_inc(last_ready, 1)

            rounds(pe, walk("tensor", {
                "turn_a0": turn_a(0), "turn_a1": turn_a(1), "turn_a2": turn_a(2),
                "turn_a3": turn_a(3), "cheb_ht": cheb_ht, "cheb_weights": cheb_weights,
                "cheb_prop3": cheb_prop3, "cheb_fold3": cheb_fold(1),
                "cheb_prop2": cheb_prop(2), "cheb_fold2": cheb_fold(2),
                "cheb_prop1": cheb_prop(3), "cheb_fold1": cheb_fold(3),
                "enc_ht": enc_ht, "encode": encode,
                **layer(0, queries=queries, keys=keys, values=values, scores0=scores(0),
                    scores1=scores(1), scores2=scores(2), turn0=turn_probs(0),
                    scores3=scores(3), turn1=turn_probs(1), turn2=turn_probs(2),
                    turn3=turn_probs(3), spread_inv=spread_inv, attend=attend),
                **layer(1, queries=queries, keys=keys, values=values),
                **layer(1, scores0=scores(0), scores1=scores(1), scores2=scores(2),
                    turn0=turn_probs(0), scores3=scores(3), turn1=turn_probs(1),
                    turn2=turn_probs(2), turn3=turn_probs(3), spread_inv=spread_inv,
                    attend=attend),
                "mlp1": mlp1, "mlp2": mlp2, "mlp3": mlp3, "gcn_prop": gcn_prop,
                "gcn_fold": gcn_fold,
                "last_prop": last_prop, "last_fold": last_fold,
            }))


_INS = ["x", "adj", "L0_gnn_weight", "L0_gnn_bias", "L1_gnn_enc_w", "L1_gnn_enc_b",
        "L1_gnn_a1_wv", "L1_gnn_a1_bv", "L1_gnn_a1_wk", "L1_gnn_a1_bk", "L1_gnn_a1_wq", "L1_gnn_a1_bq",
        "L1_gnn_a2_wv", "L1_gnn_a2_bv", "L1_gnn_a2_wk", "L1_gnn_a2_bk", "L1_gnn_a2_wq", "L1_gnn_a2_bq",
        "L1_gnn_m_w1", "L1_gnn_m_b1", "L1_gnn_m_w2", "L1_gnn_m_b2", "L1_gnn_m_w3", "L1_gnn_m_b3",
        "L2_gnn_kernel"]


def kernel(**inputs):
    import numpy as _np
    import concourse.bacc as _bacc
    from concourse import mybir as _mybir
    from concourse.bass_utils import run_bass_kernel_spmd as _run

    nc = _bacc.Bacc("TRN2", target_bir_lowering=False, num_devices=1)
    arrays, a = {}, {}
    for name in _INS:
        v = _np.ascontiguousarray(inputs[name])
        arrays[f"in_{name}"] = v
        a[name] = nc.dram_tensor(f"in_{name}", v.shape, _mybir.dt.from_np(v.dtype),
                                 kind="ExternalInput").ap()
    out = nc.dram_tensor("out_0", inputs["x"].shape, _mybir.dt.float32, kind="ExternalOutput").ap()
    att_w = [[a[f"L1_gnn_a{k}_w{s}"] for s in "vkq"] for k in (1, 2)]
    att_b = [[a[f"L1_gnn_a{k}_b{s}"] for s in "vkq"] for k in (1, 2)]
    graph_layers(nc, a["x"], a["adj"], a["L0_gnn_weight"], a["L0_gnn_bias"], a["L1_gnn_enc_w"],
                 a["L1_gnn_enc_b"], att_w, att_b, a["L1_gnn_m_w1"], a["L1_gnn_m_b1"],
                 a["L1_gnn_m_w2"], a["L1_gnn_m_b2"], a["L1_gnn_m_w3"], a["L1_gnn_m_b3"],
                 a["L2_gnn_kernel"], out)
    r = _run(nc, [arrays], core_ids=[0])
    return r.results[0]["out_0"]
```
